# Optimizing a Trainium2 kernel written in Bass

```python
import numpy as np
import jax
import jax.numpy as jnp

def _softmax(x, axis=-1):
    return jax.nn.softmax(x, axis=axis)

def _gelu(x):
    return jax.nn.gelu(x, approximate=True)

def _silu(x):
    return jax.nn.silu(x)

def _sigmoid(x):
    return jax.nn.sigmoid(x)

def _layernorm(x, axis=-1, eps=1e-05):
    m = jnp.mean(x, axis=axis, keepdims=True)
    v = jnp.var(x, axis=axis, keepdims=True)
    return (x - m) / jnp.sqrt(v + eps)

def _scatter_add(tgt, idx, src, axis=0):
    return tgt.at[idx].add(src)

def _segment_sum(src, seg, n):
    return jax.ops.segment_sum(src, seg, n)
kernel_name = 'mk_vit_tower_postln_d1_tok_img768_r4_7479bf'

def setup_inputs(seed: int=0):
    np.random.seed(seed)
    _w = jnp.asarray

    def _rec_inputs():
        import jax
        import jax.numpy as jnp
        _rk = jax.random.key(seed)
        x = -0.000348323 + 0.999952 * jax.random.normal(jax.random.fold_in(_rk, 1), (64, 96, 96, 3), jnp.float32)
        return x
    x = _rec_inputs()

    def _L0_tok_setup():
        import jax, jax.numpy as jnp
        import numpy as np

        def _extract_patches(images, p):
            B, H, W, C = images.shape
            gh, gw = (H // p, W // p)
            x = images.reshape(B, gh, p, gw, p, C)
            x = x.transpose(0, 1, 3, 2, 4, 5)
            return x.reshape(B, gh * gw, p * p * C)
        key = jax.random.key(seed)
        k1, k2, k3 = jax.random.split(key, 3)
        B, H, Wd, C = (32, 96, 96, 3)
        p = 16
        patch_dim = p * p * C
        proj_dim = 192
        num_patches = H // p * (Wd // p)
        images = jax.random.normal(k1, (B, H, Wd, C), dtype=jnp.float32)
        W = jax.random.normal(k2, (patch_dim, proj_dim), dtype=jnp.float32) * patch_dim ** (-0.5)
        b = jnp.zeros((proj_dim,), dtype=jnp.float32)
        pos_emb = jax.random.normal(k3, (num_patches, proj_dim), dtype=jnp.float32) * 0.02
        return {'images': images, 'W': W, 'b': b, 'pos_emb': pos_emb, 'patch_size': p}
    _L0_tok_all = _L0_tok_setup()
    _L0_tok_in = {k: v for k, v in _L0_tok_all.items() if k in ('W', 'b', 'pos_emb')}
    del _L0_tok_all

    def _L0_attn_setup():
        import jax, jax.numpy as jnp
        import numpy as np
        from jax import lax
        B_SZ, L, D, N, R = (1, 1024, 192, 16, 48)

        def _soft_clamp(x, lo=0.0001, hi=10.0):
            center = (hi + lo) / 2.0
            half_range = (hi - lo) / 2.0
            return center + half_range * jnp.tanh((x - center) / half_range)
        key = jax.random.key(seed)
        ks = jax.random.split(key, 6)
        x = jax.random.normal(ks[0], (B_SZ, L, D), jnp.float32)
        A_log = jnp.log(jnp.broadcast_to(jnp.arange(1, N + 1, dtype=jnp.float32), (D, N)))
        D_param = jnp.ones((D,), jnp.float32)
        W_bc = jax.random.normal(ks[1], (D, 2 * N), jnp.float32) / np.sqrt(D).astype(np.float32)
        W_dt = jax.random.normal(ks[2], (D, R), jnp.float32) / np.sqrt(D).astype(np.float32)
        W_dtp = jax.random.normal(ks[3], (R, D), jnp.float32) / np.sqrt(R).astype(np.float32)
        dt = jax.random.uniform(ks[4], (D,), jnp.float32, 0.001, 0.1)
        dt = jnp.clip(dt, 0.0001)
        b_dt = dt + jnp.log(-jnp.expm1(-dt))
        rms_scale = jnp.ones((D,), jnp.float32)
        return {'x': x, 'A_log': A_log, 'D_param': D_param, 'W_bc': W_bc, 'W_dt': W_dt, 'W_dtp': W_dtp, 'b_dt': b_dt, 'rms_scale': rms_scale}
    _L0_attn_all = _L0_attn_setup()
    _L0_attn_in = {k: v for k, v in _L0_attn_all.items() if k in ('A_log', 'D_param', 'W_bc', 'W_dt', 'W_dtp', 'b_dt', 'rms_scale')}
    del _L0_attn_all

    def _L0_ffn_setup():
        import jax, jax.numpy as jnp
        import numpy as np
        B, S, D = (2, 256, 192)
        I = 96
        E = 8
        G = 4
        TOPK_GROUPS = 2
        K = 2
        ROUTE_SCALE = 1.0
        ALPHA, LIMIT = (1.702, 7.0)

        def swiglu(h):
            xg = jnp.minimum(h[..., ::2], LIMIT)
            xl = jnp.clip(h[..., 1::2], -LIMIT, LIMIT)
            return xg * jax.nn.sigmoid(ALPHA * xg) * (xl + 1.0)

        def gate(x, gate_w, gate_b):
            scores = jax.nn.softmax(jnp.einsum('td,ed->te', x, gate_w).astype(jnp.float32), axis=-1)
            original_scores = scores
            s = scores + gate_b
            T = x.shape[0]
            sg = s.reshape(T, G, E // G)
            group_scores = jnp.sum(jax.lax.top_k(sg, 2)[0], axis=-1)
            _, gidx = jax.lax.top_k(group_scores, TOPK_GROUPS)
            keep = jnp.any(jax.nn.one_hot(gidx, G, dtype=jnp.bool_), axis=1)
            sg = jnp.where(keep[:, :, None], sg, -jnp.inf)
            s = sg.reshape(T, E)
            _, idx = jax.lax.top_k(s, K)
            w = jnp.take_along_axis(original_scores, idx, axis=1) * ROUTE_SCALE
            return (w.astype(x.dtype), idx)

        def expert_ffn(x, W1, B1, W3, B3, W2, B2):
            h1 = jnp.einsum('td,edh->teh', x, W1) + B1
            h3 = jnp.einsum('td,edh->teh', x, W3) + B3
            g = swiglu(h1 * h3)
            return jnp.einsum('tei,eid->ted', g, W2) + B2

        def shared_ffn(x, Ws1, Bs1, Ws3, Bs3, Ws2, Bs2):
            h = (x @ Ws1 + Bs1) * (x @ Ws3 + Bs3)
            return swiglu(h) @ Ws2 + Bs2
        key = jax.random.key(seed)
        ks = jax.random.split(key, 16)
        sc = 0.02
        inp = {'x': jax.random.normal(ks[0], (B, S, D), jnp.float32), 'gate_w': jax.random.normal(ks[1], (E, D), jnp.float32) * sc, 'gate_b': jax.random.normal(ks[2], (E,), jnp.float32) * sc, 'W1': jax.random.normal(ks[3], (E, D, 2 * I), jnp.float32) * sc, 'B1': jax.random.normal(ks[4], (E, 2 * I), jnp.float32) * sc, 'W3': jax.random.normal(ks[5], (E, D, 2 * I), jnp.float32) * sc, 'B3': jax.random.normal(ks[6], (E, 2 * I), jnp.float32) * sc, 'W2': jax.random.normal(ks[7], (E, I, D), jnp.float32) * sc, 'B2': jax.random.normal(ks[8], (E, D), jnp.float32) * sc, 'Ws1': jax.random.normal(ks[9], (D, 2 * I), jnp.float32) * sc, 'Bs1': jax.random.normal(ks[10], (2 * I,), jnp.float32) * sc, 'Ws3': jax.random.normal(ks[11], (D, 2 * I), jnp.float32) * sc, 'Bs3': jax.random.normal(ks[12], (2 * I,), jnp.float32) * sc, 'Ws2': jax.random.normal(ks[13], (I, D), jnp.float32) * sc, 'Bs2': jax.random.normal(ks[14], (D,), jnp.float32) * sc}
        return inp
    _L0_ffn_all = _L0_ffn_setup()
    _L0_ffn_in = {k: v for k, v in _L0_ffn_all.items() if k in ('gate_w', 'gate_b', 'W1', 'B1', 'W3', 'B3', 'W2', 'B2', 'Ws1', 'Bs1', 'Ws3', 'Bs3', 'Ws2', 'Bs2')}
    del _L0_ffn_all
    return {'x': x, 'L0_tok_W': _L0_tok_in['W'], 'L0_tok_b': _L0_tok_in['b'], 'L0_tok_pos_emb': _L0_tok_in['pos_emb'], 'L0_attn_A_log': _L0_attn_in['A_log'], 'L0_attn_D_param': _L0_attn_in['D_param'], 'L0_attn_W_bc': _L0_attn_in['W_bc'], 'L0_attn_W_dt': _L0_attn_in['W_dt'], 'L0_attn_W_dtp': _L0_attn_in['W_dtp'], 'L0_attn_b_dt': _L0_attn_in['b_dt'], 'L0_attn_rms_scale': _L0_attn_in['rms_scale'], 'L0_ffn_gate_w': _L0_ffn_in['gate_w'], 'L0_ffn_gate_b': _L0_ffn_in['gate_b'], 'L0_ffn_W1': _L0_ffn_in['W1'], 'L0_ffn_B1': _L0_ffn_in['B1'], 'L0_ffn_W3': _L0_ffn_in['W3'], 'L0_ffn_B3': _L0_ffn_in['B3'], 'L0_ffn_W2': _L0_ffn_in['W2'], 'L0_ffn_B2': _L0_ffn_in['B2'], 'L0_ffn_Ws1': _L0_ffn_in['Ws1'], 'L0_ffn_Bs1': _L0_ffn_in['Bs1'], 'L0_ffn_Ws3': _L0_ffn_in['Ws3'], 'L0_ffn_Bs3': _L0_ffn_in['Bs3'], 'L0_ffn_Ws2': _L0_ffn_in['Ws2'], 'L0_ffn_Bs2': _L0_ffn_in['Bs2']}

def reference(x, L0_tok_W, L0_tok_b, L0_tok_pos_emb, L0_attn_A_log, L0_attn_D_param, L0_attn_W_bc, L0_attn_W_dt, L0_attn_W_dtp, L0_attn_b_dt, L0_attn_rms_scale, L0_ffn_gate_w, L0_ffn_gate_b, L0_ffn_W1, L0_ffn_B1, L0_ffn_W3, L0_ffn_B3, L0_ffn_W2, L0_ffn_B2, L0_ffn_Ws1, L0_ffn_Bs1, L0_ffn_Ws3, L0_ffn_Bs3, L0_ffn_Ws2, L0_ffn_Bs2):
    import jax
    import jax.numpy as jnp

    def _L0_tok_ref(images, W, b, pos_emb, patch_size):
        import jax, jax.numpy as jnp
        import numpy as np

        def _extract_patches(images, p):
            B, H, W, C = images.shape
            gh, gw = (H // p, W // p)
            x = images.reshape(B, gh, p, gw, p, C)
            x = x.transpose(0, 1, 3, 2, 4, 5)
            return x.reshape(B, gh * gw, p * p * C)
        patches = _extract_patches(images, patch_size)
        out = jnp.einsum('bnd,de->bne', patches, W) + b + pos_emb
        return out

    def _L0_attn_ref(x, A_log, D_param, W_bc, W_dt, W_dtp, b_dt, rms_scale):
        import jax, jax.numpy as jnp
        import numpy as np
        from jax import lax
        B_SZ, L, D, N, R = (1, 1024, 192, 16, 48)

        def _soft_clamp(x, lo=0.0001, hi=10.0):
            center = (hi + lo) / 2.0
            half_range = (hi - lo) / 2.0
            return center + half_range * jnp.tanh((x - center) / half_range)
        n = A_log.shape[1]
        A = -jnp.exp(A_log)
        bc = x @ W_bc
        B_sel, C_sel = (bc[..., :n], bc[..., n:])
        delta = jax.nn.softplus(x @ W_dt @ W_dtp + b_dt)
        delta = delta * lax.rsqrt(jnp.mean(delta * delta, axis=-1, keepdims=True) + 1e-06) * rms_scale
        delta = _soft_clamp(delta, 0.0001, 10.0)
        dE = delta[..., None]
        half = 0.5 * dE * A
        denom = 1.0 - half
        A_bar = (1.0 + half) / denom
        B_bar = jnp.sqrt(dE) * B_sel[:, :, None, :] / denom
        x_prev = jnp.concatenate([jnp.zeros_like(x[:, :1]), x[:, :-1]], axis=1)
        x_in = 0.5 * (x + x_prev)
        Bx = B_bar * x_in[..., None]

        def op(left, right):
            a_l, b_l = left
            a_r, b_r = right
            return (a_r * a_l, a_r * b_l + b_r)
        _, all_h = lax.associative_scan(op, (A_bar, Bx), axis=1)
        y = jnp.sum(C_sel[:, :, None, :] * all_h, axis=-1)
        return y + D_param * x

    def _L0_ffn_ref(x, gate_w, gate_b, W1, B1, W3, B3, W2, B2, Ws1, Bs1, Ws3, Bs3, Ws2, Bs2):
        import jax, jax.numpy as jnp
        import numpy as np
        B, S, D = (2, 256, 192)
        I = 96
        E = 8
        G = 4
        TOPK_GROUPS = 2
        K = 2
        ROUTE_SCALE = 1.0
        ALPHA, LIMIT = (1.702, 7.0)

        def swiglu(h):
            xg = jnp.minimum(h[..., ::2], LIMIT)
            xl = jnp.clip(h[..., 1::2], -LIMIT, LIMIT)
            return xg * jax.nn.sigmoid(ALPHA * xg) * (xl + 1.0)

        def gate(x, gate_w, gate_b):
            scores = jax.nn.softmax(jnp.einsum('td,ed->te', x, gate_w).astype(jnp.float32), axis=-1)
            original_scores = scores
            s = scores + gate_b
            T = x.shape[0]
            sg = s.reshape(T, G, E // G)
            group_scores = jnp.sum(jax.lax.top_k(sg, 2)[0], axis=-1)
            _, gidx = jax.lax.top_k(group_scores, TOPK_GROUPS)
            keep = jnp.any(jax.nn.one_hot(gidx, G, dtype=jnp.bool_), axis=1)
            sg = jnp.where(keep[:, :, None], sg, -jnp.inf)
            s = sg.reshape(T, E)
            _, idx = jax.lax.top_k(s, K)
            w = jnp.take_along_axis(original_scores, idx, axis=1) * ROUTE_SCALE
            return (w.astype(x.dtype), idx)

        def expert_ffn(x, W1, B1, W3, B3, W2, B2):
            h1 = jnp.einsum('td,edh->teh', x, W1) + B1
            h3 = jnp.einsum('td,edh->teh', x, W3) + B3
            g = swiglu(h1 * h3)
            return jnp.einsum('tei,eid->ted', g, W2) + B2

        def shared_ffn(x, Ws1, Bs1, Ws3, Bs3, Ws2, Bs2):
            h = (x @ Ws1 + Bs1) * (x @ Ws3 + Bs3)
            return swiglu(h) @ Ws2 + Bs2
        inp_shape = x.shape
        xt = x.reshape(-1, D)
        w, idx = gate(xt, gate_w, gate_b)
        combine = jnp.einsum('tk,tke->te', w, jax.nn.one_hot(idx, E, dtype=w.dtype))
        per_expert = expert_ffn(xt, W1, B1, W3, B3, W2, B2)
        routed = jnp.einsum('ted,te->td', per_expert, combine)
        out = routed + shared_ffn(xt, Ws1, Bs1, Ws3, Bs3, Ws2, Bs2)
        return out.reshape(inp_shape)
    h = _L0_tok_ref(x, L0_tok_W, L0_tok_b, L0_tok_pos_emb, 16)
    h = _layernorm(h + _L0_attn_ref(h, L0_attn_A_log, L0_attn_D_param, L0_attn_W_bc, L0_attn_W_dt, L0_attn_W_dtp, L0_attn_b_dt, L0_attn_rms_scale), axis=-1)
    h = _layernorm(h + _L0_ffn_ref(h, L0_ffn_gate_w, L0_ffn_gate_b, L0_ffn_W1, L0_ffn_B1, L0_ffn_W3, L0_ffn_B3, L0_ffn_W2, L0_ffn_B2, L0_ffn_Ws1, L0_ffn_Bs1, L0_ffn_Ws3, L0_ffn_Bs3, L0_ffn_Ws2, L0_ffn_Bs2), axis=-1)
    return h

_drawn_inputs = setup_inputs


def setup_inputs(seed=0):
    import zlib

    import numpy as np

    out = dict(_drawn_inputs(seed))
    spreads = {'L0_tok_b': (0.0, 0.1), 'L0_attn_D_param': (1.0, 0.2), 'L0_attn_rms_scale': (1.0, 0.6)}
    factors = {'L0_ffn_gate_w': 8.0,
     'L0_ffn_gate_b': 8.0,
     'L0_ffn_W1': 8.0,
     'L0_ffn_B1': 8.0,
     'L0_ffn_W3': 8.0,
     'L0_ffn_B3': 8.0,
     'L0_ffn_W2': 8.0,
     'L0_ffn_B2': 61.501,
     'L0_ffn_Ws1': 7.311,
     'L0_ffn_Bs1': 8.0,
     'L0_ffn_Ws3': 7.325,
     'L0_ffn_Bs3': 8.0,
     'L0_ffn_Ws2': 7.256,
     'L0_ffn_Bs2': 23.752}
    for name, (base, spread) in spreads.items():
        noise = np.random.default_rng([zlib.crc32(name.encode()), seed]).standard_normal(out[name].shape)
        drawn = base * np.exp(spread * noise) if base else spread * noise
        out[name] = jnp.asarray(drawn.astype(out[name].dtype))
    for name, factor in factors.items():
        out[name] = (out[name] * factor).astype(out[name].dtype)
    return out
```

```python
from contextlib import ExitStack

import concourse.bass as bass
from concourse import mybir

F32 = mybir.dt.float32
BF16 = mybir.dt.bfloat16
ALU = mybir.AluOpType
ACT = mybir.ActivationFunctionType
AX = mybir.AxisListType

IMAGES, PATCHES, D, STATES = 64, 36, 192, 16
D0, D1 = 128, 64
DT_RANK = 48
EXPERTS, HID = 8, 96
SLOT = PATCHES + 1
OCT = 8
OCTS = IMAGES // OCT
W = OCT * SLOT
TOK = OCT * PATCHES
KC = 6
PAIRS = STATES // 2
TT = 96
TILES = IMAGES * PATCHES // 128
NE = EXPERTS + 1
GRP = 3
GRPS = NE // GRP
GK = NE * HID + EXPERTS + 1
GC = -(-GK // 128)
GLAST = GK - (GC - 1) * 128
LO_CLAMP, HI_CLAMP = 0.0001, 10.0
CENTER, HALF = (HI_CLAMP + LO_CLAMP) / 2.0, (HI_CLAMP - LO_CLAMP) / 2.0
LN2 = 0.6931471805599453
BIG = 1e30
CREDIT, CREDIT_DMA = 1, 16

V_ALOW, V_AHIGH, V_BDT, V_RMS, V_D, V_TB, V_N = 0, 16, 24, 26, 28, 30, 32


def vit_tower(nc, patches, w_tok, vecs, pos, w_bc, w_dt, w_dtp, ident, pair_ident, bc_pick, ones_row,
              gate_w, gate_b, below, w13_low, w13_high, w2, out):
    with ExitStack() as ctx:
        def sb(name, shape, dt=F32):
            return ctx.enter_context(nc.sbuf_tensor(name, shape, dt))

        def sem(name):
            return ctx.enter_context(nc.semaphore(name))

        psum = ctx.enter_context(nc.psum_tensor("psum", [128, 8, 512], F32))
        patches_v = patches.rearrange("o p c w -> p o c w")
        out_v = out.rearrange("i s n -> (i s) n").rearrange("(t p) n -> p t n", p=128)
        flat = psum[:, :, :].rearrange("p b n -> p (b n)")

        w_tok_sb = sb("w_tok_sb", [128, KC, 256])
        vec = sb("vec", [128, V_N])
        pos_sb = sb("pos_sb", [128, 2, SLOT])
        w_bc_sb = sb("w_bc_sb", [128, 2, 96])
        w_dt_sb = sb("w_dt_sb", [128, 2, DT_RANK])
        w_dtp_sb = sb("w_dtp_sb", [DT_RANK, 256])
        id_sb = sb("id_sb", [128, 128])
        pair_sb = sb("pair_sb", [128, 64])
        pick_sb = sb("pick_sb", [96, 34])
        ones_sb = sb("ones_sb", [128, 128])
        sel = sb("sel", [96, 48, 128], BF16)
        bias_low = sb("bias_low", [128, STATES])
        bias_high = sb("bias_high", [128, PAIRS])
        one_plus_d = sb("one_plus_d", [128, 2])
        gate_w_sb = sb("gate_w_sb", [128, 2, EXPERTS])
        gate_b_sb = sb("gate_b_sb", [128, EXPERTS])
        below_sb = sb("below_sb", [128, EXPERTS, EXPERTS])
        w13l = sb("w13l", [128, NE, 4 * HID])
        w13h = sb("w13h", [D1 + 1, NE, 4 * HID])
        w2_sb = sb("w2_sb", [128, GC, D])
        clamp_bias = sb("clamp_bias", [128, 1])
        idle = sb("idle", [1, 12])
        mv_eps = sb("mv_eps", [TT, 3])
        oeps = sb("oeps", [128, 2])
        minus_half = sb("minus_half", [128, TT])

        patch_sb = sb("patch_sb", [128, 2, KC, W])
        xt = sb("xt", [128, 2, W])
        xsum = sb("xsum", [128, 2, W])
        bc1 = sb("bc1", [96, W], BF16)
        bct = sb("bct", [96, W])
        bc2 = sb("bc2", [96, W], BF16)
        bcs = sb("bcs", [96, W], BF16)
        low = sb("low", [DT_RANK, W])
        za = sb("za", [128, 2, W])
        ze = sb("ze", [128, 2, W])
        dl = sb("dl", [128, 2, W])
        ms = sb("ms", [128, W])
        rs = sb("rs", [128, W])
        rt = sb("rt", [128, W])
        lnd = sb("lnd", [128, 2, W])
        u = sb("u", [128, 3, W])
        abar = sb("abar", [128, 2, 3, W])
        v = sb("v", [128, 3, W])
        bx = sb("bx", [128, 3, W])
        h = sb("h", [128, 3, W])
        ch = sb("ch", [128, 2, 3, W])
        res = sb("res", [128, 2, TOK])
        st6 = sb("st6", [TT, 3, 6])
        mv = sb("mv", [TT, 3, 2])
        rstd = sb("rstd", [TT, 3])
        hn = sb("hn", [TT, 3, D])

        hlow = sb("hlow", [128, OCTS * TOK])
        hhigh = sb("hhigh", [D1 + 1, OCTS * TOK])

        T8 = [128, TILES, EXPERTS]
        prob = sb("prob", T8)
        score = sb("score", T8)
        keep8 = sb("keep8", T8)
        cmpa = sb("cmpa", [128, TILES, EXPERTS, EXPERTS])
        cmpb = sb("cmpb", [128, TILES, EXPERTS, EXPERTS])
        g4 = sb("g4", [128, TILES, 4])
        r4 = sb("r4", [128, TILES, 4])
        k4 = sb("k4", [128, TILES, 4])
        row = sb("row", [128, TILES])
        wt = sb("wt", [128, 2, NE])
        comb = sb("comb", [128, TILES, NE])
        hl = sb("hl", [128, 2, 128])
        hh = sb("hh", [D1 + 1, 2, 128])
        h3 = sb("h3", [128, 2, GRP, 2 * HID])
        prod = sb("prod", [128, 2, 2, GRP * HID])
        xg = sb("xg", [128, 2, GRP * HID])
        xl = sb("xl", [128, 2, GRP * HID])
        sg = sb("sg", [128, 2, GRP * HID])
        xa = sb("xa", [128, 2, GRP * HID])
        g = sb("g", [128, 2, GC * 128])
        gt = sb("gt", [128, GC, 128])
        o6 = sb("o6", [128, 6])
        omv = sb("omv", [128, 2, 2])
        orstd = sb("orstd", [128, 2])
        ot = sb("ot", [128, 2, D])

        s_w1, s_w2, s_patch = sem("weights1_in"), sem("weights2_in"), [sem("patch_in0"), sem("patch_in1")]
        s_setup, s_vec = sem("setup_done"), sem("setup_step")
        s_idle = sem("idle_set")
        s_relu, s_wt = sem("relu_ready"), sem("weights_staged")
        s_emb, s_xt = sem("embedded"), sem("xt_ready")
        s_xsum = sem("xsum_ready")
        s_bc, s_bcsplit, s_bcact = sem("bc_product"), sem("bc_split_vec"), sem("bc_split_act")
        s_low, s_lows = sem("low_product"), sem("low_ready")
        s_z, s_sp, s_spv, s_sq = sem("z_product"), sem("softplus_act"), sem("softplus_vec"), sem("square_ready")
        s_ms, s_msact, s_rms = sem("meansq_product"), sem("meansq_act"), sem("rms_vec")
        s_tanh, s_clamp, s_lnd, s_u = sem("clamp_tanh"), sem("clamp_done"), sem("log_delta"), sem("u_ready")
        s_a, s_b, s_c = sem("abar_ready"), sem("b_bcast"), sem("c_bcast")
        s_v, s_bx, s_h, s_ch = sem("v_ready"), sem("bx_ready"), sem("h_ready"), sem("ch_ready")
        s_y = sem("y_added")
        s_res, s_rtr, s_stat, s_rstd, s_hn = (sem("res_ready"), sem("res_turned"), sem("stat_step"),
                                              sem("rstd_ready"), sem("hn_ready"))
        s_htr, s_hout = sem("hn_turned"), sem("h_stored")
        s_gl, s_gs, s_gx, s_comb = sem("gate_logits"), sem("gate_step"), sem("gate_exp"), sem("combine_ready")
        s_stage, s_hid, s_h3, s_prod = sem("tile_staged"), sem("hidden_ready"), sem("h3_copied"), sem("prod_ready")
        s_clip, s_sig, s_xa, s_g = sem("clipped"), sem("sigmoid_ready"), sem("xa_ready"), sem("g_ready")
        s_gtr, s_gt, s_op = sem("g_turned"), sem("gt_copied"), sem("out_product")
        s_ostat, s_orstd, s_ot, s_out = sem("out_stat"), sem("out_rstd"), sem("out_tile"), sem("out_stored")

        block = ctx.enter_context(nc.Block())

        N_W1, N_W2 = 9, 7

        @block.sync
        def _(sp):
            for dst, src in ((w_tok_sb, w_tok), (vec, vecs), (pos_sb, pos), (w_bc_sb, w_bc), (w_dt_sb, w_dt),
                             (w_dtp_sb, w_dtp), (id_sb, ident), (pair_sb, pair_ident), (pick_sb, bc_pick)):
                sp.dma_start(dst[:], src).then_inc(s_w1, 16)
            sp.dma_start(patch_sb[:, 0:1], patches_v[:, 0:1]).then_inc(s_patch[0], 16)
            for dst, src in ((gate_w_sb, gate_w), (gate_b_sb, gate_b), (below_sb, below), (w13l, w13_low),
                             (w13h, w13_high), (w2_sb, w2)):
                sp.dma_start(dst[:], src).then_inc(s_w2, 16)
            sp.dma_start(hhigh[D1:D1 + 1, :], ones_row[:, :]).then_inc(s_w2, 16)
            sp.dma_start(patch_sb[:, 1:2], patches_v[:, 1:2]).then_inc(s_patch[1], 16)
            with sp.Fori(0, OCTS // 2 - 1) as o2:
                for par in range(2):
                    sp.wait_ge(s_emb, (o2 * 2 + par + 1) * 2)
                    sp.dma_start(patch_sb[:, par:par + 1],
                                 patches_v[:, bass.ds(o2 * 2 + 2 + par, 1)]).then_inc(s_patch[par], 16)
            with sp.Fori(0, TILES // 2) as t2:
                for par in range(2):
                    sp.wait_ge(s_ot, CREDIT + t2 * 2 + par + 1)
                    sp.dma_start(out_v[:, bass.ds(t2 * 2 + par, 1), :], ot[:, par:par + 1, :]).then_inc(s_out, 16)
            sp.wait_ge(s_out, CREDIT_DMA + 16 * TILES)

        def images(ap):
            return ap.rearrange("p (i s) -> p i s", s=SLOT)

        @block.tensor
        def _(pe):
            def bank(b, p, n, off=0):
                return psum[0:p, b, off:off + n]

            pe.wait_ge(s_w1, 16 * N_W1)
            pe.wait_ge(s_setup, 1)
            with pe.Fori(0, OCTS // 2) as o2:
                for par in range(2):
                    o = o2 * 2 + par
                    pe.wait_ge(s_patch[par], (o2 + 1) * 16)
                    pe.wait_ge(s_res, CREDIT + o * 2)
                    for half in range(2):
                        for c in range(KC):
                            mm = nc.tensor.matmul(bank(4 + half, 128, W), w_tok_sb[:, c, half * 128:half * 128 + 128],
                                                  patch_sb[:, par, c, :], start=(c == 0), stop=(c == KC - 1))
                        mm.then_inc(s_emb, 1)
                    pe.wait_ge(s_xt, (o + 1) * 2)
                    pe.wait_ge(s_hout, CREDIT + o * 2)
                    nc.tensor.matmul(bank(6, DT_RANK, W), w_dt_sb[:, 0, :], xt[:, 0, :], start=True, stop=False)
                    nc.tensor.matmul(bank(6, DT_RANK, W), w_dt_sb[0:D1, 1, :], xt[0:D1, 1, :], start=False,
                                     stop=True).then_inc(s_low, 1)
                    nc.tensor.matmul(bank(7, 96, W), w_bc_sb[:, 0, :], xt[:, 0, :], start=True, stop=False)
                    nc.tensor.matmul(bank(7, 96, W), w_bc_sb[0:D1, 1, :], xt[0:D1, 1, :], start=False,
                                     stop=True).then_inc(s_bc, 1)
                    pe.wait_ge(s_lows, o + 1)
                    for half in range(2):
                        mm = nc.tensor.matmul(bank(2 + half, 128, W), w_dtp_sb[:, half * 128:half * 128 + 128],
                                              low[:, :], start=True, stop=True)
                    mm.then_inc(s_z, 1)
                    pe.wait_ge(s_sq, o + 1)
                    nc.tensor.matmul(bank(6, 128, W), ones_sb[:, :], ze[:, 0, :], start=True, stop=False)
                    nc.tensor.matmul(bank(6, 128, W), ones_sb[0:D1, :], ze[0:D1, 1, :], start=False,
                                     stop=True).then_inc(s_ms, 1)

                    def broadcast(m, first, b0):
                        for seg, c0, c1 in ((0, 0, W), (1, W, 512), (1, 512, 2 * W), (2, 2 * W, 3 * W)):
                            col = first + 2 * m + seg if seg < 2 else 32 + first // 2 + m
                            mm = nc.tensor.matmul(flat[:, b0 * 512 + c0:b0 * 512 + c1], sel[:, col, :],
                                                  bcs[:, c0 - seg * W:c1 - seg * W], start=True, stop=True)
                        return mm

                    def add_states(m):
                        pe.wait_ge(s_ch, o * PAIRS + m + 1)
                        for k in range(2):
                            nc.tensor.matmul(bank(4, 128, W), id_sb[:, :], ch[:, m % 2, k, :],
                                             start=(m == 0 and k == 0), stop=(m == PAIRS - 1 and k == 1))
                        nc.tensor.matmul(bank(5, 64, W), pair_sb[:, :], ch[:, m % 2, 2, :], start=(m == 0),
                                         stop=(m == PAIRS - 1)).then_inc(s_y, 1)

                    pe.wait_ge(s_bcsplit, (o + 1) * 2)
                    for m in range(PAIRS):
                        if m:
                            pe.wait_ge(s_v, o * PAIRS + m)
                        broadcast(m, 0, 0).then_inc(s_b, 1)
                        if m == 0:
                            pe.wait_ge(s_spv, (o + 1) * 1)
                        else:
                            pe.wait_ge(s_ch, o * PAIRS + m)
                        broadcast(m, 16, 2).then_inc(s_c, 1)
                        if m:
                            add_states(m - 1)
                    add_states(PAIRS - 1)

                    pe.wait_ge(s_res, CREDIT + (o + 1) * 2)
                    for t in range(3):
                        dst = lambda a, b: psum[0:TT, 6 + t // 2, (t % 2) * D + a:(t % 2) * D + b]
                        nc.tensor.transpose(dst(0, D0), res[:, 0, t * TT:(t + 1) * TT], id_sb[:, :])
                        nc.tensor.transpose(dst(D0, D), res[0:D1, 1, t * TT:(t + 1) * TT],
                                            id_sb[0:D1, 0:D1]).then_inc(s_rtr, 1)
                    pe.wait_ge(s_hn, (o + 1) * 3)
                    for t in range(3):
                        mm = nc.tensor.transpose(psum[0:D0, 6, t * TT:(t + 1) * TT], hn[:, t, 0:D0], id_sb[0:TT, 0:TT])
                    mm.then_inc(s_htr, 1)
                    for t in range(3):
                        mm = nc.tensor.transpose(psum[0:D1, 7, t * TT:(t + 1) * TT], hn[:, t, D0:D], id_sb[0:TT, 0:TT])
                    mm.then_inc(s_htr, 1)

            pe.wait_ge(s_w2, 16 * N_W2)
            pe.wait_ge(s_hout, CREDIT + OCTS * 2)
            for t in range(TILES):
                nc.tensor.matmul(psum[:, 6, t * EXPERTS:(t + 1) * EXPERTS], hlow[:, t * 128:(t + 1) * 128],
                                 gate_w_sb[:, 0, :], start=True, stop=False)
                mm = nc.tensor.matmul(psum[:, 6, t * EXPERTS:(t + 1) * EXPERTS], hhigh[0:D1, t * 128:(t + 1) * 128],
                                      gate_w_sb[0:D1, 1, :], start=False, stop=True)
            mm.then_inc(s_gl, 1)
            pe.wait_ge(s_gs, 1)

            with pe.Fori(0, TILES // 2) as t2:
                for par in range(2):
                    t = t2 * 2 + par
                    pe.wait_ge(s_stage, t + 1)
                    for q in range(GRPS):
                        n = par * GRPS + q
                        b0 = (n % 2) * GRP
                        if q >= 2 or par:
                            pe.wait_ge(s_prod, CREDIT + t * GRPS + q - 1)
                        else:
                            pe.wait_ge(s_prod, CREDIT + (t * GRPS + q - 1 if q else t2 * (2 * GRPS)))
                        for e in range(GRP):
                            x = q * GRP + e
                            nc.tensor.matmul(psum[:, b0 + e, 0:4 * HID], hl[:, par, :], w13l[:, x, :],
                                             start=True, stop=False)
                            mm = nc.tensor.matmul(psum[:, b0 + e, 0:4 * HID], hh[:, par, :], w13h[:, x, :],
                                                  start=False, stop=True)
                        mm.then_inc(s_hid, 1)
                    pe.wait_ge(s_g, t * GRPS + GRPS)
                    for c in range(GC):
                        n = 128 if c < GC - 1 else GLAST
                        if c == 4:
                            pe.wait_ge(s_gt, CREDIT + t * 2 + 1)
                        if c == 0:
                            pe.wait_ge(s_gt, CREDIT + t * 2)
                        mm = nc.tensor.transpose(psum[0:n, 6, (c % 4) * 128:(c % 4 + 1) * 128],
                                                 g[:, par, c * 128:c * 128 + n], id_sb[:, :])
                        if c in (3, GC - 1):
                            mm.then_inc(s_gtr, 1)
                    pe.wait_ge(s_ot, CREDIT + t)
                    nc.tensor.matmul(psum[:, 7, 0:D0], hl[:, par, :], id_sb[:, :], start=True, stop=False,
                                     skip_group_check=True)
                    nc.tensor.matmul(psum[:, 7, D0:D], hh[0:D1, par, :], id_sb[0:D1, 0:D1], start=False, stop=False,
                                     skip_group_check=True)
                    for c in range(GC):
                        n = 128 if c < GC - 1 else GLAST
                        if c in (0, 4):
                            pe.wait_ge(s_gt, CREDIT + t * 2 + 1 + c // 4)
                        mm = nc.tensor.matmul(psum[:, 7, 0:D], gt[0:n, c, :], w2_sb[0:n, c, :], start=False,
                                              stop=(c == GC - 1), skip_group_check=True)
                    mm.then_inc(s_op, 1)

        @block.scalar
        def _(act):
            act.wait_ge(s_setup, 1)
            with act.Fori(0, OCTS) as o:
                def fn(out, in_, f, s=None, **kw):
                    i = nc.scalar.activation(out, in_, f, **kw)
                    return i.then_inc(s, 1) if s is not None else i

                act.wait_ge(s_low, o + 1)
                fn(low[:, :], psum[0:DT_RANK, 6, 0:W], ACT.Copy, s_lows)
                act.wait_ge(s_bc, o + 1)
                fn(bc1[:, :], psum[0:96, 7, 0:W], ACT.Copy, s_bcact)
                act.wait_ge(s_bcsplit, o * 2 + 1)
                fn(bc2[:, :], bct[:, :], ACT.Copy, s_bcact)
                act.wait_ge(s_z, o + 1)
                for k in range(2):
                    fn(za[:, k, :], psum[:, 2 + k, 0:W], ACT.Abs, s_sp, bias=vec[:, V_BDT + k:V_BDT + k + 1])
                act.wait_ge(s_sp, o * 4 + 2)
                fn(ze[:, :, :], za[:, :, :], ACT.Exp, s_sp, scale=-1.0)
                act.wait_ge(s_sp, o * 4 + 3)
                fn(dl[:, :, :], ze[:, :, :], ACT.Ln, s_sp, bias=1.0)
                act.wait_ge(s_spv, o + 1)
                act.wait_ge(s_sp, o * 4 + 4)
                fn(ze[:, :, :], dl[:, :, :], ACT.Square, s_sq)
                act.wait_ge(s_ms, o + 1)
                act.wait_ge(s_rms, o * 7 + 1)
                fn(rt[:, :], ms[:, :], ACT.Ln, s_msact)
                act.wait_ge(s_msact, o * 2 + 1)
                fn(rs[:, :], rt[:, :], ACT.Exp, s_msact, scale=-0.5)
                act.wait_ge(s_rms, o * 7 + 7)
                fn(za[:, :, :], dl[:, :, :], ACT.Tanh, s_tanh, scale=1.0 / HALF, bias=clamp_bias[:, 0:1])
                act.wait_ge(s_clamp, o + 1)
                fn(lnd[:, :, :], dl[:, :, :], ACT.Ln, s_lnd)
                act.wait_ge(s_lnd, o * 2 + 1)
                fn(za[:, :, :], lnd[:, :, :], ACT.Exp, s_lnd, scale=0.5)
                for m in range(PAIRS):
                    if m >= 2:
                        act.wait_ge(s_h, o * PAIRS + m - 1)
                    for k in range(3):
                        b = bias_low[:, 2 * m + k:2 * m + k + 1] if k < 2 else bias_high[:, m:m + 1]
                        i = fn(images(abar[:, m % 2, k, :])[:, :, 1:], images(lnd[:, k // 2, :])[:, :, 1:],
                               ACT.Tanh, None, scale=-0.5, bias=b)
                    i.then_inc(s_a, 1)
                act.wait_ge(s_htr, o * 2 + 1)
                fn(hlow[:, bass.ds(o * TOK, TOK)], psum[:, 6, 0:TOK], ACT.Copy, s_hout)
                act.wait_ge(s_htr, o * 2 + 2)
                fn(hhigh[0:D1, bass.ds(o * TOK, TOK)], psum[0:D1, 7, 0:TOK], ACT.Copy, s_hout)

            act.wait_ge(s_gs, 3)
            nc.scalar.activation(prob[:, :, :], score[:, :, :], ACT.Exp).then_inc(s_gx, 1)

            with act.Fori(0, TILES // 2) as t2:
                for par in range(2):
                    t = t2 * 2 + par
                    for q in range(GRPS):
                        n = par * GRPS + q
                        b0 = (n % 2) * GRP
                        act.wait_ge(s_hid, t * GRPS + q + 1)
                        nc.scalar.activation(h3[:, n % 2], psum[:, b0:b0 + GRP, 2 * HID:4 * HID],
                                             ACT.Copy).then_inc(s_h3, 1)
                        act.wait_ge(s_clip, (t * GRPS + q) * 2 + 1)
                        nc.scalar.activation(sg[:, n % 2, :], xg[:, n % 2, :], ACT.Sigmoid,
                                             scale=1.702).then_inc(s_sig, 1)
                    act.wait_ge(s_gtr, CREDIT + t * 2 + 1)
                    act.wait_ge(s_op, CREDIT + t)
                    nc.scalar.activation(gt[:, 0:4, :], psum[:, 6, 0:512].rearrange("p (c n) -> p c n", n=128),
                                         ACT.Copy).then_inc(s_gt, 1)
                    act.wait_ge(s_gtr, CREDIT + t * 2 + 2)
                    nc.scalar.activation(gt[:, 4:6, :], psum[:, 6, 0:256].rearrange("p (c n) -> p c n", n=128),
                                         ACT.Copy)
                    nc.scalar.activation(gt[0:GLAST, 6, :], psum[0:GLAST, 6, 256:384], ACT.Copy).then_inc(s_gt, 1)

        @block.gpsimd
        def _(pool):
            with pool.Fori(0, OCTS) as o:
                pool.wait_ge(s_stat, (o + 1) * 7)
                nc.gpsimd.tensor_tensor(rstd[:, :], mv_eps[:, :], minus_half[0:TT, 0:3], ALU.pow).then_inc(s_rstd, 1)
            pool.wait_ge(s_hout, CREDIT + OCTS * 2)
            pool.wait_ge(s_w2, 16 * N_W2)
            with pool.Fori(0, TILES // 2) as t2:
                pool.wait_ge(s_op, CREDIT + t2 * 2)
                for par in range(2):
                    t = t2 * 2 + par
                    nc.gpsimd.tensor_copy(hl[:, par, :], hlow[:, bass.ds(t * 128, 128)])
                    nc.gpsimd.tensor_copy(hh[:, par, :], hhigh[:, bass.ds(t * 128, 128)]).then_inc(s_stage, 1)
                for par in range(2):
                    t = t2 * 2 + par
                    pool.wait_ge(s_ostat, (t + 1) * 3)
                    nc.gpsimd.tensor_tensor(orstd[:, par:par + 1], oeps[:, par:par + 1], minus_half[:, 0:1],
                                            ALU.pow).then_inc(s_orstd, 1)

        @block.vector
        def _(dve):
            V = nc.vector
            for i, credited in enumerate((s_res, s_hout, s_prod, s_gt, s_ot, s_op, s_gtr, s_idle)):
                V.memset(idle[0:1, 1 + i:2 + i], 0.0).then_inc(credited, CREDIT)
            V.memset(idle[0:1, 9:10], 0.0).then_inc(s_out, CREDIT_DMA)
            V.memset(ones_sb[:, :], 1.0)
            V.memset(minus_half[:, :], -0.5)
            V.memset(abar[:, :, :, :], 0.0)
            V.memset(clamp_bias[:, :], -CENTER / HALF).then_inc(s_vec, 1)
            dve.wait_ge(s_w1, 16 * N_W1)
            V.tensor_scalar(bias_low[:, :], vec[:, V_ALOW:V_ALOW + STATES], LN2, -0.5, ALU.subtract, ALU.mult)
            V.tensor_scalar(bias_high[:, :], vec[:, V_AHIGH:V_AHIGH + PAIRS], LN2, -0.5, ALU.subtract, ALU.mult)
            V.tensor_scalar(one_plus_d[:, :], vec[:, V_D:V_D + 2], 1.0, None, ALU.add)
            for k in range(2):
                V.tensor_scalar(pos_sb[:, k, 1:], pos_sb[:, k, 1:], vec[:, V_TB + k:V_TB + k + 1], None, ALU.add)
            V.tensor_copy(sel[:, 0:32, :], pick_sb[:, 0:32].unsqueeze(2).to_broadcast([96, 32, 128]))
            V.tensor_copy(sel[:, 32:48, 0:64], pick_sb[:, 0:32:2].unsqueeze(2).to_broadcast([96, 16, 64]))
            V.tensor_copy(sel[:, 32:48, 64:128],
                          pick_sb[:, 1:32:2].unsqueeze(2).to_broadcast([96, 16, 64])).then_inc(s_setup, 1)
            dve.wait_ge(s_setup, 1)

            with dve.Fori(0, OCTS) as o:
                for k in range(2):
                    dve.wait_ge(s_emb, o * 2 + k + 1)
                    V.tensor_tensor(images(xt[:, k, :]), images(psum[:, 4 + k, 0:W]),
                                    pos_sb[:, k, :].unsqueeze(1).to_broadcast([128, OCT, SLOT]),
                                    ALU.add).then_inc(s_xt, 1)
                dve.wait_ge(s_xt, o * 2 + 2)
                for k in range(2):
                    V.tensor_copy(xsum[:, k, 0:1], xt[:, k, 0:1])
                    i = V.tensor_tensor(xsum[:, k, 1:], xt[:, k, 1:], xt[:, k, :W - 1], ALU.add)
                i.then_inc(s_xsum, 1)
                dve.wait_ge(s_bcact, o * 2 + 1)
                V.scalar_tensor_tensor(out=bct[:, :], in0=bc1[:, :], scalar=pick_sb[:, 32:33], in1=psum[0:96, 7, 0:W],
                                       op0=ALU.mult, op1=ALU.add).then_inc(s_bcsplit, 1)
                dve.wait_ge(s_bcact, o * 2 + 2)
                dve.wait_ge(s_bcsplit, o * 2 + 1)
                V.scalar_tensor_tensor(out=bcs[:, :], in0=bc2[:, :], scalar=pick_sb[:, 33:34], in1=bct[:, :],
                                       op0=ALU.mult, op1=ALU.add).then_inc(s_bcsplit, 1)
                dve.wait_ge(s_sp, o * 4 + 4)
                for k in range(2):
                    i = V.tensor_scalar(za[:, k, :], psum[:, 2 + k, 0:W], vec[:, V_BDT + k:V_BDT + k + 1], 0.0,
                                    ALU.add, ALU.max)
                i.then_inc(s_relu, 1)
                dve.wait_ge(s_relu, o + 1)
                V.tensor_tensor(dl[:, :, :], dl[:, :, :], za[:, :, :], ALU.add).then_inc(s_spv, 1)
                dve.wait_ge(s_ms, o + 1)
                V.tensor_scalar(ms[:, :], psum[:, 6, 0:W], 1.0 / D, 1e-6, ALU.mult, ALU.add).then_inc(s_rms, 1)
                dve.wait_ge(s_msact, o * 2 + 2)
                V.tensor_tensor(rt[:, :], rs[:, :], rs[:, :], ALU.mult).then_inc(s_rms, 1)
                dve.wait_ge(s_rms, o * 7 + 2)
                V.tensor_tensor(rt[:, :], rt[:, :], ms[:, :], ALU.mult).then_inc(s_rms, 1)
                dve.wait_ge(s_rms, o * 7 + 3)
                V.tensor_scalar(rt[:, :], rt[:, :], -0.5, 1.5, ALU.mult, ALU.add).then_inc(s_rms, 1)
                dve.wait_ge(s_rms, o * 7 + 4)
                V.tensor_tensor(rs[:, :], rs[:, :], rt[:, :], ALU.mult).then_inc(s_rms, 1)
                dve.wait_ge(s_rms, o * 7 + 5)
                for k in range(2):
                    V.scalar_tensor_tensor(out=dl[:, k, :], in0=dl[:, k, :], scalar=vec[:, V_RMS + k:V_RMS + k + 1],
                                           in1=rs[:, :], op0=ALU.mult, op1=ALU.mult).then_inc(s_rms, 1)
                dve.wait_ge(s_tanh, o + 1)
                V.tensor_scalar(dl[:, :, :], za[:, :, :], HALF, CENTER, ALU.mult, ALU.add).then_inc(s_clamp, 1)
                dve.wait_ge(s_lnd, o * 2 + 2)
                dve.wait_ge(s_xsum, o + 1)
                for k in range(3):
                    i = V.scalar_tensor_tensor(out=u[:, k, :], in0=xsum[:, k // 2, :], scalar=0.25,
                                               in1=za[:, k // 2, :], op0=ALU.mult, op1=ALU.mult)
                i.then_inc(s_u, 1)
                dve.wait_ge(s_u, o + 1)

                n0 = o * PAIRS
                bank_b = flat[:, 0:3 * W]
                bank_c = flat[:, 1024:1024 + 3 * W]

                def f3(t):
                    return t.rearrange("p a b -> p (a b)")

                def make_v(m):
                    dve.wait_ge(s_b, n0 + m + 1)
                    if m:
                        dve.wait_ge(s_bx, n0 + m)
                    V.tensor_tensor(f3(v[:, :, :]), f3(u[:, :, :]), bank_b, ALU.mult).then_inc(s_v, 1)

                def make_bx(m):
                    dve.wait_ge(s_a, n0 + m + 1)
                    dve.wait_ge(s_v, n0 + m + 1)
                    V.scalar_tensor_tensor(out=f3(bx[:, :, :]), in0=f3(abar[:, m % 2]), scalar=1.0,
                                           in1=f3(v[:, :, :]), op0=ALU.add, op1=ALU.mult).then_inc(s_bx, 1)

                make_v(0)
                make_bx(0)
                for m in range(PAIRS):
                    dve.wait_ge(s_bx, n0 + m + 1)
                    V.tensor_tensor_scan(f3(h[:, :, :]), f3(abar[:, m % 2]), f3(bx[:, :, :]), 0.0,
                                         ALU.mult, ALU.add).then_inc(s_h, 1)
                    if m + 1 < PAIRS:
                        make_v(m + 1)
                    dve.wait_ge(s_h, n0 + m + 1)
                    dve.wait_ge(s_c, n0 + m + 1)
                    if m >= 2:
                        dve.wait_ge(s_y, n0 + m - 1)
                    V.tensor_tensor(f3(ch[:, m % 2]), f3(h[:, :, :]), bank_c, ALU.mult).then_inc(s_ch, 1)
                    if m + 1 < PAIRS:
                        make_bx(m + 1)
                dve.wait_ge(s_y, n0 + PAIRS)
                for k, p in ((0, 128), (1, 64)):
                    V.scalar_tensor_tensor(out=res[0:p, k, :].rearrange("p (i s) -> p i s", s=PATCHES),
                                           in0=images(xt[0:p, k, :])[:, :, 1:], scalar=one_plus_d[0:p, k:k + 1],
                                           in1=images(psum[0:p, 4 + k, 0:W])[:, :, 1:],
                                           op0=ALU.mult, op1=ALU.add).then_inc(s_res, 1)
                tile = lambda t: psum[0:TT, 6 + t // 2, (t % 2) * D:(t % 2) * D + D]
                for t in range(3):
                    dve.wait_ge(s_rtr, o * 3 + (2 if t < 2 else 3))
                    V.bn_stats(st6[:, t, :], tile(t)).then_inc(s_stat, 1)
                dve.wait_ge(s_idle, CREDIT + o)
                dve.wait_ge(s_stat, o * 7 + 3)
                V.memset(idle[0:1, 0:1], 0.0).then_inc(s_idle, 1)
                for t in range(3):
                    i = V.bn_aggr(mv[:, t, :], st6[:, t, :]).then_inc(s_stat, 1)
                dve.wait_ge(s_stat, o * 7 + 6)
                V.tensor_scalar(mv_eps[:, :], mv[:, :, 1], 1e-5, None, ALU.add).then_inc(s_stat, 1)
                dve.wait_ge(s_rstd, o + 1)
                for t in range(3):
                    V.tensor_scalar(hn[:, t, :], tile(t), mv[:, t, 0:1], rstd[:, t:t + 1],
                                    ALU.subtract, ALU.mult).then_inc(s_hn, 1)

            steps = [0]

            def step(i):
                steps[0] += 1
                i.then_inc(s_gs, 1)
                dve.wait_ge(s_gs, steps[0])

            B3 = [128, TILES, EXPERTS]
            dve.wait_ge(s_gl, 1)
            step(V.tensor_copy(keep8[:, :, :], psum[:, 6, 0:TILES * EXPERTS].rearrange("p (t e) -> p t e", e=EXPERTS)))
            step(V.tensor_reduce(row[:, :], keep8[:, :, :], AX.X, ALU.max))
            step(V.tensor_tensor(score[:, :, :], keep8[:, :, :], row[:, :].unsqueeze(2).to_broadcast(B3), ALU.subtract))
            dve.wait_ge(s_gx, 1)
            step(V.tensor_reduce(row[:, :], prob[:, :, :], AX.X, ALU.add))
            step(V.reciprocal(row[:, :], row[:, :]))
            step(V.tensor_tensor(prob[:, :, :], prob[:, :, :], row[:, :].unsqueeze(2).to_broadcast(B3), ALU.mult))
            step(V.tensor_tensor(score[:, :, :], prob[:, :, :],
                                 gate_b_sb[:, :].unsqueeze(1).to_broadcast(B3), ALU.add))
            step(V.tensor_tensor(g4[:, :, :], score[:, :, 0::2], score[:, :, 1::2], ALU.add))

            def rank(dst, s, n):
                mine = s.unsqueeze(3).to_broadcast([128, TILES, n, n])
                other = s.unsqueeze(2).to_broadcast([128, TILES, n, n])
                a, b = cmpa[:, :, 0:n, 0:n], cmpb[:, :, 0:n, 0:n]
                step(V.tensor_tensor(a, other, mine, ALU.is_equal))
                step(V.tensor_tensor(a, a, below_sb[:, 0:n, 0:n].unsqueeze(1).to_broadcast([128, TILES, n, n]),
                                     ALU.mult))
                step(V.tensor_tensor(b, other, mine, ALU.is_gt))
                step(V.tensor_tensor(a, a, b, ALU.add))
                step(V.tensor_reduce(dst, a, AX.X, ALU.add))

            rank(r4[:, :, :], g4[:, :, :], 4)
            step(V.tensor_scalar(k4[:, :, :], r4[:, :, :], 2.0, None, ALU.is_lt))
            step(V.tensor_scalar(r4[:, :, :], k4[:, :, :], BIG, -BIG, ALU.mult, ALU.add))
            for k in range(2):
                step(V.tensor_tensor(score[:, :, k::2], score[:, :, k::2], r4[:, :, :], ALU.add))
            rank(keep8[:, :, :], score[:, :, :], EXPERTS)
            step(V.tensor_scalar(keep8[:, :, :], keep8[:, :, :], 2.0, None, ALU.is_lt))
            V.memset(comb[:, :, EXPERTS:NE], 1.0)
            step(V.tensor_tensor(comb[:, :, 0:EXPERTS], keep8[:, :, :], prob[:, :, :], ALU.mult))

            with dve.Fori(0, TILES // 2) as t2:
                for par in range(2):
                    t = t2 * 2 + par
                    V.tensor_copy(wt[:, par, :], comb[:, bass.ds(t, 1), :].rearrange("p o e -> p (o e)")
                                  ).then_inc(s_wt, 1)
                    dve.wait_ge(s_wt, t + 1)
                    dve.wait_ge(s_gtr, CREDIT + t2 * 4)
                    V.tensor_copy(g[:, par, NE * HID:GK], wt[:, par, :])
                    for q in range(GRPS):
                        n = par * GRPS + q
                        b0 = (n % 2) * GRP
                        k = t * GRPS + q
                        dve.wait_ge(s_h3, k + 1)
                        hid = h3[:, n % 2].rearrange("p e (w i) -> p e w i", w=2)
                        V.tensor_tensor(prod[:, n % 2].rearrange("p w (e i) -> p e w i", e=GRP),
                                        psum[:, b0:b0 + GRP, 0:2 * HID].rearrange("p e (w i) -> p e w i", w=2),
                                        hid, ALU.mult).then_inc(s_prod, 1)
                        dve.wait_ge(s_prod, CREDIT + k + 1)
                        V.tensor_scalar(xg[:, n % 2, :], prod[:, n % 2, 0, :], 7.0, None, ALU.min).then_inc(s_clip, 1)
                        V.tensor_scalar(xl[:, n % 2, :], prod[:, n % 2, 1, :], -7.0, 7.0, ALU.max,
                                        ALU.min).then_inc(s_clip, 1)
                        dve.wait_ge(s_clip, k * 2 + 2)
                        V.scalar_tensor_tensor(out=xa[:, n % 2, :], in0=xl[:, n % 2, :], scalar=1.0,
                                               in1=xg[:, n % 2, :], op0=ALU.add, op1=ALU.mult).then_inc(s_xa, 1)
                        dve.wait_ge(s_xa, k + 1)
                        dve.wait_ge(s_sig, k + 1)
                        for e in range(GRP):
                            x = q * GRP + e
                            i = V.scalar_tensor_tensor(out=g[:, par, x * HID:(x + 1) * HID],
                                                       in0=xa[:, n % 2, e * HID:(e + 1) * HID],
                                                       scalar=wt[:, par, x:x + 1],
                                                       in1=sg[:, n % 2, e * HID:(e + 1) * HID],
                                                       op0=ALU.mult, op1=ALU.mult)
                        i.then_inc(s_g, 1)
                    dve.wait_ge(s_op, CREDIT + t + 1)
                    V.bn_stats(o6[:, :], psum[:, 7, 0:D]).then_inc(s_ostat, 1)
                    dve.wait_ge(s_ostat, t * 3 + 1)
                    dve.wait_ge(s_idle, CREDIT + t + OCTS)
                    V.memset(idle[0:1, 0:1], 0.0).then_inc(s_idle, 1)
                    V.bn_aggr(omv[:, par, :], o6[:, :]).then_inc(s_ostat, 1)
                    dve.wait_ge(s_ostat, t * 3 + 2)
                    V.tensor_scalar(oeps[:, par:par + 1], omv[:, par, 1:2], 1e-5, None, ALU.add).then_inc(s_ostat, 1)
                    dve.wait_ge(s_orstd, t + 1)
                    dve.wait_ge(s_out, CREDIT_DMA + t2 * 32)
                    V.tensor_scalar(ot[:, par, :], psum[:, 7, 0:D], omv[:, par, 0:1], orstd[:, par:par + 1],
                                    ALU.subtract, ALU.mult).then_inc(s_ot, 1)


def kernel(**inputs):
    import numpy as _np
    import concourse.bacc as _bacc
    from concourse import mybir as _mybir
    from concourse.bass_utils import run_bass_kernel_spmd as _run

    x = {k: _np.asarray(a) for k, a in inputs.items()}

    def padded(a, shape):
        z = _np.zeros(shape, a.dtype)
        z[tuple(slice(0, n) for n in a.shape)] = a
        return z

    def low_high(a, twice=False):
        z = _np.zeros((128, 2, a.shape[1]), a.dtype)
        z[:, 0], z[:D1, 1] = a[:D0], a[D0:]
        if twice:
            z[D1:, 1] = a[D0:]
        return z

    im = x["x"].reshape(OCTS, OCT, 6, 16, 6, 48).transpose(0, 3, 5, 1, 2, 4).reshape(OCTS, KC, 128, OCT, PATCHES)
    patches = _np.zeros((OCTS, 128, KC, OCT, SLOT), im.dtype)
    patches[..., 1:] = im.transpose(0, 2, 1, 3, 4)
    patches = patches.reshape(OCTS, 128, KC, W)
    wt = x["L0_tok_W"].reshape(KC, 128, D).transpose(1, 0, 2)
    w_tok = _np.concatenate([wt, wt[:, :, D0:]], axis=2)
    col = lambda n: low_high(x[n][:, None], True)[:, :, 0]
    a_log = low_high(x["L0_attn_A_log"], True)
    a_high = _np.concatenate([a_log[:D1, 1, 0::2], a_log[:D1, 1, 1::2]], axis=0)
    vecs = _np.concatenate([a_log[:, 0], a_high, col("L0_attn_b_dt"), col("L0_attn_rms_scale"),
                            col("L0_attn_D_param"), col("L0_tok_b")], axis=1)
    pos = _np.zeros((128, 2, SLOT), _np.float32)
    pos[:, :, 1:] = low_high(_np.ascontiguousarray(x["L0_tok_pos_emb"].T), True)
    w_bc = low_high(_np.concatenate([x["L0_attn_W_bc"]] * 3, axis=1))
    w_dt = low_high(x["L0_attn_W_dt"])
    w_dtp = _np.concatenate([x["L0_attn_W_dtp"], x["L0_attn_W_dtp"][:, D0:]], axis=1)
    ident = _np.eye(128, dtype=_np.float32)
    pair_ident = _np.concatenate([ident[:D1, :D1]] * 2, axis=0)
    pick = _np.zeros((96, 34), _np.float32)
    pick[:, :32] = _np.concatenate([ident[:32, :32]] * 3, axis=0)
    pick[32:, 32] = -1.0
    pick[64:, 33] = -1.0
    gate_w = low_high(_np.ascontiguousarray(x["L0_ffn_gate_w"].T))
    gate_b = _np.ascontiguousarray(_np.broadcast_to(x["L0_ffn_gate_b"], (128, EXPERTS)))
    below = _np.ascontiguousarray(_np.broadcast_to(_np.tri(EXPERTS, EXPERTS, -1, dtype=_np.float32),
                                                   (128, EXPERTS, EXPERTS)))

    def halves(w, ws):
        w = _np.concatenate([w, ws[None]], axis=0)
        return _np.concatenate([w[..., 0::2], w[..., 1::2]], axis=-1)

    w13 = _np.concatenate([halves(x["L0_ffn_W1"], x["L0_ffn_Ws1"]), halves(x["L0_ffn_W3"], x["L0_ffn_Ws3"])], axis=-1)
    b13 = _np.concatenate([halves(x["L0_ffn_B1"], x["L0_ffn_Bs1"]), halves(x["L0_ffn_B3"], x["L0_ffn_Bs3"])], axis=-1)
    w13 = _np.concatenate([w13, b13[:, None]], axis=1).transpose(1, 0, 2)
    w2 = _np.concatenate([x["L0_ffn_W2"].reshape(-1, D), x["L0_ffn_Ws2"], x["L0_ffn_B2"], x["L0_ffn_Bs2"][None]], axis=0)
    w2 = padded(w2, (GC * 128, D)).reshape(GC, 128, D).transpose(1, 0, 2)
    laid = {"patches": patches, "w_tok": w_tok, "vecs": vecs, "pos": pos, "w_bc": w_bc, "w_dt": w_dt, "w_dtp": w_dtp,
            "ident": ident, "pair_ident": pair_ident, "bc_pick": pick,
            "ones_row": _np.ones((1, OCTS * TOK), _np.float32), "gate_w": gate_w, "gate_b": gate_b,
            "below": below, "w13_low": w13[:128], "w13_high": w13[128:], "w2": w2}

    nc = _bacc.Bacc("TRN2", target_bir_lowering=False, num_devices=1)
    arrays, args = {}, []
    for name, a in laid.items():
        a = _np.ascontiguousarray(a)
        arrays[f"in_{name}_dram"] = a
        args.append(nc.dram_tensor(f"in_{name}_dram", a.shape, _mybir.dt.from_np(a.dtype), kind="ExternalInput").ap())
    out = nc.dram_tensor("out_0_dram", (IMAGES, PATCHES, D), _mybir.dt.float32, kind="ExternalOutput").ap()
    vit_tower(nc, *args, out)
    r = _run(nc, [arrays], core_ids=[0])
    return r.results[0]["out_0_dram"]
```

```python
from contextlib import ExitStack

import concourse.bass as bass
from concourse import mybir

F32 = mybir.dt.float32
BF16 = mybir.dt.bfloat16
F32R = mybir.dt.float32r
ALU = mybir.AluOpType
ACT = mybir.ActivationFunctionType
AX = mybir.AxisListType

IMAGES, PATCHES, D, STATES = 64, 36, 192, 16
D0, D1 = 128, 64
DT_RANK = 48
EXPERTS, HID = 8, 96
SLOT = PATCHES + 1
OCT = 8
OCTS = IMAGES // OCT
W = OCT * SLOT
TOK = OCT * PATCHES
KC = 6
PAIRS = STATES // 2
AB = 4
TILES = IMAGES * PATCHES // 128
NE = EXPERTS + 1
GRP = 3
GRPS = NE // GRP
GK = NE * HID + EXPERTS + 1
GC = -(-GK // 128)
GLAST = GK - (GC - 1) * 128
LO_CLAMP, HI_CLAMP = 0.0001, 10.0
CENTER, HALF = (HI_CLAMP + LO_CLAMP) / 2.0, (HI_CLAMP - LO_CLAMP) / 2.0
LN2 = 0.6931471805599453
BIG = 1e30
LOOPED = OCTS - 2
CREDIT, CREDIT_DMA, AB_CREDIT, Y_CREDIT = 1, 16, AB, 2

V_ALOW, V_AHIGH, V_BDT, V_RMS, V_D, V_TB, V_BIAS, V_TAIL, V_N = 0, 16, 24, 26, 28, 30, 32, 33, 34


def vit_tower(nc, patches, w_tok, vecs, pos, w_bc, w_dt, w_dtp, ident, pair_ident, bc_pick,
              gate_w, gate_b, below, w13_low, w13_tail, w13_rest, w2, out):
    with ExitStack() as ctx:
        def sb(name, shape, dt=F32):
            return ctx.enter_context(nc.sbuf_tensor(name, shape, dt))

        def sem(name):
            return ctx.enter_context(nc.semaphore(name))

        psum = ctx.enter_context(nc.psum_tensor("psum", [128, 8, 512], F32))
        patches_v = patches.rearrange("o p c w -> p o c w")
        out_v = out.rearrange("i s n -> (i s) n").rearrange("(t p) n -> p t n", p=128)
        flat = psum[:, :, :].rearrange("p b n -> p (b n)")

        w_tok_sb = sb("w_tok_sb", [128, KC, 256])
        vec = sb("vec", [128, V_N])
        pos_sb = sb("pos_sb", [128, 2, SLOT])
        w_bc_sb = sb("w_bc_sb", [128, 2, 96])
        w_dt_sb = sb("w_dt_sb", [128, 2, DT_RANK])
        w_dtp_sb = sb("w_dtp_sb", [DT_RANK, 256])
        id_sb = sb("id_sb", [128, 128])
        pair_sb = sb("pair_sb", [128, 64])
        pick_sb = sb("pick_sb", [96, 34])
        ones_sb = sb("ones_sb", [128, 128])
        sel = sb("sel", [96, 48, 128], BF16)
        bias_low = sb("bias_low", [128, STATES])
        bias_high = sb("bias_high", [128, PAIRS])
        one_plus_d = sb("one_plus_d", [128, 2])
        gate_w_sb = sb("gate_w_sb", [128, 2, EXPERTS])
        gate_b_sb = sb("gate_b_sb", [128, EXPERTS])
        below_sb = sb("below_sb", [128, EXPERTS, EXPERTS])
        w_hi = sb("w_hi", [128, NE, 4 * HID], F32R)
        w_lo = sb("w_lo", [128, NE, 4 * HID], F32R)
        wt_hi = sb("wt_hi", [128, NE, 4 * HID], F32R)
        wt_lo = sb("wt_lo", [D1 + 2, NE, 4 * HID], F32R)
        gate_r = sb("gate_r", [128, 4, EXPERTS], F32R)
        id_r = sb("id_r", [128, 128], F32R)
        pair_r = sb("pair_r", [128, D1], F32R)
        w2_sb = sb("w2_sb", [128, GC, D])
        ms_eps = sb("ms_eps", [128, 1])
        center = sb("center", [128, 1])
        clamp_bias = sb("clamp_bias", [128, 1])
        idle = sb("idle", [1, 16])
        oeps = sb("oeps", [128, 2])
        minus_half = sb("minus_half", [128, 2])

        res_low = sb("res_low", [128, OCTS * TOK])
        res_high = sb("res_high", [D1, OCTS * TOK])

        scan_space = ExitStack()

        def scan_sb(name, shape, dt=F32):
            return scan_space.enter_context(nc.sbuf_tensor(name, shape, dt))

        patch_sb = scan_sb("patch_sb", [128, 2, KC, W])
        xt = scan_sb("xt", [128, 2, 2, W])
        xsum = scan_sb("xsum", [128, 2, W])
        bc1 = scan_sb("bc1", [96, W], BF16)
        bct = scan_sb("bct", [96, W])
        bc2 = scan_sb("bc2", [96, W], BF16)
        bcs = scan_sb("bcs", [96, 2, W], BF16)
        low = scan_sb("low", [DT_RANK, W])
        za = scan_sb("za", [128, 2, W])
        zr = scan_sb("zr", [128, 2, W])
        ze = scan_sb("ze", [128, 2, W])
        dl = scan_sb("dl", [128, 2, W])
        rs = scan_sb("rs", [128, W])
        rt = scan_sb("rt", [128, W])
        lnd = scan_sb("lnd", [128, 2, 2, W])
        u = scan_sb("u", [128, 2, 3, W])
        abar = scan_sb("abar", [128, AB, 3, W])
        v = scan_sb("v", [128, 3, W])
        bx = scan_sb("bx", [128, 3, W])
        h = scan_sb("h", [128, 3, W])
        ch = scan_sb("ch", [128, 2, 3, W])
        raw_low = scan_sb("raw_low", [128, GRP, 4 * HID])
        raw_tail = scan_sb("raw_tail", [128, GRP, 4 * HID])
        raw_rest = scan_sb("raw_rest", [D1 + 2, GRP, 4 * HID])
        rest_hi = scan_sb("rest_hi", [D1 + 2, GRP, 4 * HID], F32R)
        diag_d = scan_sb("diag_d", [128, 2, 128])

        scan_space.close()

        h_hi = sb("h_hi", [128, OCTS * TOK], F32R)
        h_lo = sb("h_lo", [128, OCTS * TOK], F32R)
        h_tail = sb("h_tail", [128, OCTS * TOK], F32R)

        rl = sb("rl", [128, 2, 128])
        rh = sb("rh", [D1, 2, 128])
        st6 = sb("st6", [128, 2, 6])
        mv = sb("mv", [128, 2, 2])
        mv_eps = sb("mv_eps", [128, 2])
        rstd = sb("rstd", [128, 2])
        hn = sb("hn", [128, 2, D + D1])
        tail_hi = sb("tail_hi", [128, 2, 128], F32R)

        T8 = [128, TILES, EXPERTS]
        prob = sb("prob", T8)
        score = sb("score", T8)
        keep8 = sb("keep8", T8)
        cmpa = sb("cmpa", [128, TILES, EXPERTS, EXPERTS])
        cmpb = sb("cmpb", [128, TILES, EXPERTS, EXPERTS])
        g4 = sb("g4", [128, TILES, 4])
        r4 = sb("r4", [128, TILES, 4])
        k4 = sb("k4", [128, TILES, 4])
        row = sb("row", [128, TILES])
        wt = sb("wt", [128, 2, NE])
        comb = sb("comb", [128, TILES, NE])
        sh_hi = sb("sh_hi", [128, 2, 128], F32R)
        sh_lo = sb("sh_lo", [128, 2, 128], F32R)
        sh_tail = sb("sh_tail", [128, 2, 128], F32R)
        sh_rest = sb("sh_rest", [D1 + 2, 2, 128], F32R)
        h3 = sb("h3", [128, 2, GRP, 2 * HID])
        prod = sb("prod", [128, 2, 2, GRP * HID])
        xg = sb("xg", [128, 2, GRP * HID])
        xl = sb("xl", [128, 2, GRP * HID])
        sg = sb("sg", [128, 2, GRP * HID])
        xa = sb("xa", [128, 2, GRP * HID])
        g = sb("g", [128, 2, GC * 128])
        gt = sb("gt", [128, GC, 128])
        o6 = sb("o6", [128, 6])
        omv = sb("omv", [128, 2, 2])
        orstd = sb("orstd", [128, 2])
        ot = sb("ot", [128, 2, D])

        s_w1, s_w2, s_patch = sem("weights1_in"), sem("weights2_in"), [sem("patch_in0"), sem("patch_in1")]
        s_setup, s_vec = sem("setup_done"), sem("setup_step")
        s_idle = sem("idle_set")
        s_relu, s_wt = sem("relu_ready"), sem("weights_staged")
        s_emb, s_xt = sem("embedded"), sem("xt_ready")
        s_xsum = sem("xsum_ready")
        s_bc, s_bcsplit, s_bcact = sem("bc_product"), sem("bc_split_vec"), sem("bc_split_act")
        s_low, s_lows = sem("low_product"), sem("low_ready")
        s_z, s_sp, s_spv, s_sq = sem("z_product"), sem("softplus_act"), sem("softplus_vec"), sem("square_ready")
        s_ucopy = sem("u_third_ready")
        s_raw, s_whi, s_wlo, s_resid = sem("raw_weights_in"), sem("weights_hi"), sem("weights_lo"), sem("residual_in")
        s_gate = sem("gate_weights_split")
        s_rest1, s_tailv = sem("ones_rows_set"), sem("tail_split")
        s_hcopy = sem("h_hi_ready")
        s_turn, s_ln, s_lnback = sem("res_staged"), sem("ln_step"), sem("hn_turned_back")
        s_ms, s_msact, s_rms = sem("meansq_product"), sem("meansq_act"), sem("rms_vec")
        s_tanh, s_clamp, s_lnd, s_u = sem("clamp_tanh"), sem("clamp_done"), sem("log_delta"), sem("u_ready")
        s_a, s_b, s_c = sem("abar_ready"), sem("b_bcast"), sem("c_bcast")
        s_v, s_bx, s_h, s_ch = sem("v_ready"), sem("bx_ready"), sem("h_ready"), sem("ch_ready")
        s_y = sem("y_added")
        s_res, s_rtr, s_stat, s_rstd, s_hn = (sem("res_ready"), sem("res_turned"), sem("stat_step"),
                                              sem("rstd_ready"), sem("hn_ready"))
        s_htr, s_hout = sem("hn_turned"), sem("h_stored")
        s_gl, s_gs, s_gx, s_comb = sem("gate_logits"), sem("gate_step"), sem("gate_exp"), sem("combine_ready")
        s_stage, s_hid, s_h3, s_prod = sem("tile_staged"), sem("hidden_ready"), sem("h3_copied"), sem("prod_ready")
        s_clip, s_sig, s_xa, s_g = sem("clipped"), sem("sigmoid_ready"), sem("xa_ready"), sem("g_ready")
        s_gtr, s_gt, s_op = sem("g_turned"), sem("gt_copied"), sem("out_product")
        s_ostat, s_orstd, s_ot, s_out = sem("out_stat"), sem("out_rstd"), sem("out_tile"), sem("out_stored")

        block = ctx.enter_context(nc.Block())

        N_W1, N_W2 = 9, 4

        @block.sync
        def _(sp):
            for dst, src in ((w_tok_sb, w_tok), (vec, vecs), (pos_sb, pos), (w_bc_sb, w_bc), (w_dt_sb, w_dt),
                             (w_dtp_sb, w_dtp), (id_sb, ident), (pair_sb, pair_ident), (pick_sb, bc_pick)):
                sp.dma_start(dst[:], src).then_inc(s_w1, 16)
            sp.dma_start(patch_sb[:, 0:1], patches_v[:, 0:1]).then_inc(s_patch[0], 16)
            sp.dma_start(patch_sb[:, 1:2], patches_v[:, 1:2]).then_inc(s_patch[1], 16)
            for dst, src in ((gate_w_sb, gate_w), (gate_b_sb, gate_b), (below_sb, below), (w2_sb, w2)):
                sp.dma_start(dst[:], src).then_inc(s_w2, 16)

            def raw_weights(q):
                for dst, src in ((raw_low, w13_low), (raw_tail, w13_tail), (raw_rest, w13_rest)):
                    sp.dma_start(dst[:], src[q]).then_inc(s_raw, 16)

            raw_weights(0)
            with sp.Fori(0, OCTS // 2 - 1) as o2:
                for par in range(2):
                    sp.wait_ge(s_emb, (o2 * 2 + par + 1) * 2)
                    sp.dma_start(patch_sb[:, par:par + 1],
                                 patches_v[:, bass.ds(o2 * 2 + 2 + par, 1)]).then_inc(s_patch[par], 16)
            for q in range(1, GRPS):
                sp.wait_ge(s_wlo, q * 2)
                raw_weights(q)
            with sp.Fori(0, TILES // 2) as t2:
                for par in range(2):
                    sp.wait_ge(s_ot, CREDIT + t2 * 2 + par + 1)
                    sp.dma_start(out_v[:, bass.ds(t2 * 2 + par, 1), :], ot[:, par:par + 1, :]).then_inc(s_out, 16)
            sp.wait_ge(s_out, CREDIT_DMA + 16 * TILES)

        def images(ap):
            return ap.rearrange("p (i s) -> p i s", s=SLOT)

        @block.tensor
        def _(pe):
            def bank(b, p, n, off=0):
                return psum[0:p, b, off:off + n]

            def embed(x, par, uses, first, last, after=True):
                for i in range(first, last):
                    half, c = i // KC, i % KC
                    if i == 0:
                        pe.wait_ge(s_patch[par], (uses + 1) * 16)
                        if after:
                            pe.wait_ge(s_bcsplit, x * 2 - 1)
                    if i == KC and after:
                        pe.wait_ge(s_rms, x * 5 - 3)
                    mm = nc.tensor.matmul(bank(7 - half, 128, W), w_tok_sb[:, c, half * 128:half * 128 + 128],
                                          patch_sb[:, par, c, :], start=(c == 0), stop=(c == KC - 1))
                    if c == KC - 1:
                        mm.then_inc(s_emb, 1)

            def project(x, par, part):
                lo, hi = xt[:, par, 0, :], xt[0:D1, par, 1, :]
                if part == 0:
                    pe.wait_ge(s_xt, (x + 1) * 2)
                    nc.tensor.matmul(bank(6, DT_RANK, W), w_dt_sb[:, 0, :], lo, start=True, stop=False)
                    nc.tensor.matmul(bank(6, DT_RANK, W), w_dt_sb[0:D1, 1, :], hi, start=False,
                                     stop=True).then_inc(s_low, 1)
                if part == 1:
                    pe.wait_ge(s_lows, x + 1)
                    for half in range(2):
                        nc.tensor.matmul(bank(7 - half, 128, W), w_dtp_sb[:, half * 128:half * 128 + 128], low[:, :],
                                         start=True, stop=True).then_inc(s_z, 1)
                if part == 2:
                    pe.wait_ge(s_sp, x * 6 + 4)
                    nc.tensor.matmul(bank(7, 96, W), w_bc_sb[:, 0, :], lo, start=True, stop=False)
                    nc.tensor.matmul(bank(7, 96, W), w_bc_sb[0:D1, 1, :], hi, start=False,
                                     stop=True).then_inc(s_bc, 1)
                if part == 3:
                    pe.wait_ge(s_sq, x + 1)
                    nc.tensor.matmul(bank(6, 128, W), ones_sb[:, :], ze[:, 0, :], start=True, stop=False)
                    nc.tensor.matmul(bank(6, 128, W), ones_sb[0:D1, :], ze[0:D1, 1, :], start=False,
                                     stop=True).then_inc(s_ms, 1)

            def broadcast(m, par, first, b0):
                for seg, c0, c1 in ((0, 0, W), (1, W, 512), (1, 512, 2 * W), (2, 2 * W, 3 * W)):
                    col = first + 2 * m + seg if seg < 2 else 32 + first // 2 + m
                    mm = nc.tensor.matmul(flat[:, b0 * 512 + c0:b0 * 512 + c1], sel[:, col, :],
                                          bcs[:, par, c0 - seg * W:c1 - seg * W], start=True, stop=True)
                return mm

            def add_states(o, par, m):
                if m == 0:
                    pe.wait_ge(s_res, CREDIT + o * 2)
                    nc.tensor.matmul(bank(4, 128, W), diag_d[:, 0, :], xt[:, par, 0, :], start=True, stop=False)
                    nc.tensor.matmul(bank(5, 64, W), diag_d[0:D1, 1, 0:D1], xt[0:D1, par, 1, :], start=True,
                                     stop=False)
                pe.wait_ge(s_ch, CREDIT + o * PAIRS + m + 1)
                for k in range(2):
                    nc.tensor.matmul(bank(4, 128, W), id_sb[:, :], ch[:, m % 2, k, :], start=False,
                                     stop=(m == PAIRS - 1 and k == 1))
                nc.tensor.matmul(bank(5, 64, W), pair_sb[:, :], ch[:, m % 2, 2, :], start=False,
                                 stop=(m == PAIRS - 1)).then_inc(s_y, 1)

            def octet(o, par, uses, next_states, next_tokens):
                for m in range(PAIRS):
                    if m + 1 < PAIRS or next_states:
                        pe.wait_ge(s_v, o * PAIRS + m + 1)
                        if m + 1 == PAIRS:
                            pe.wait_ge(s_bcsplit, (o + 2) * 2)
                        broadcast((m + 1) % PAIRS, (par + (m + 1) // PAIRS) % 2, 0, 0).then_inc(s_b, 1)
                    pe.wait_ge(s_ch, CREDIT + o * PAIRS + m)
                    broadcast(m, par, 16, 2).then_inc(s_c, 1)
                    if next_states and m == 0:
                        project(o + 1, 1 - par, 0)
                    if next_states and m == 2:
                        project(o + 1, 1 - par, 2)
                    if next_states and m == 3:
                        project(o + 1, 1 - par, 3)
                    if next_tokens and m in EMBED_A:
                        embed(o + 2, par, uses + 1, *EMBED_A[m])
                    if m:
                        add_states(o, par, m - 1)
                    if next_states and m == 0:
                        project(o + 1, 1 - par, 1)
                    if next_tokens and m in EMBED_B:
                        embed(o + 2, par, uses + 1, *EMBED_B[m])
                add_states(o, par, PAIRS - 1)

            EMBED_A = {4: (0, 2), 5: (3, 5), 6: (6, 8), 7: (10, 12)}
            EMBED_B = {4: (2, 3), 5: (5, 6), 6: (8, 10)}

            pe.wait_ge(s_w1, 16 * N_W1)
            pe.wait_ge(s_setup, 1)
            embed(0, 0, 0, 0, 2 * KC, after=False)
            for part in range(4):
                project(0, 0, part)
            embed(1, 1, 0, 0, 2 * KC)
            pe.wait_ge(s_bcsplit, 2)
            broadcast(0, 0, 0, 0).then_inc(s_b, 1)
            with pe.Fori(0, LOOPED // 2) as o2:
                for par in range(2):
                    octet(o2 * 2 + par, par, o2, True, True)
            octet(OCTS - 2, 0, OCTS // 2 - 1, True, False)
            octet(OCTS - 1, 1, OCTS // 2 - 1, False, False)

            with pe.Fori(0, TILES // 2) as t2:
                for par in range(2):
                    t = t2 * 2 + par
                    pe.wait_ge(s_turn, t + 1)
                    pe.wait_ge(s_hn, CREDIT + t2 * 2)
                    nc.tensor.transpose(psum[:, par, 0:D0], rl[:, par, :], id_sb[:, :])
                    nc.tensor.transpose(psum[:, par, D0:D], rh[:, par, :], id_sb[0:D1, 0:D1]).then_inc(s_rtr, 1)
                for par in range(2):
                    t = t2 * 2 + par
                    pe.wait_ge(s_hn, CREDIT + t + 1)
                    pe.wait_ge(s_hout, CREDIT + t2 * 2)
                    nc.tensor.transpose(psum[:, 2 + par, 0:128], hn[:, par, 0:D0], id_sb[:, :])
                    nc.tensor.transpose(psum[:, 4 + par, 0:128], hn[:, par, D0:D + D1], id_sb[:, :]).then_inc(s_htr, 1)

            pe.wait_ge(s_gate, 4)
            pe.wait_ge(s_w2, 16 * N_W2)
            pe.wait_ge(s_hout, CREDIT + TILES)
            for t in range(TILES):
                cols = slice(t * 128, (t + 1) * 128)
                for i, (part, w) in enumerate(((h_hi, 0), (h_hi, 1), (h_lo, 0), (h_tail, 2), (h_tail, 3))):
                    mm = nc.tensor.matmul(psum[:, 6, t * EXPERTS:(t + 1) * EXPERTS], part[:, cols], gate_r[:, w, :],
                                          start=(i == 0), stop=(i == 4))
            mm.then_inc(s_gl, 1)

            def hidden(t, par, q):
                b0 = (par + q) % 2 * GRP
                if not (isinstance(t, int) and t * GRPS + q < 2):
                    pe.wait_ge(s_prod, t * GRPS + q - 1)
                for i, (a, w) in enumerate(((sh_hi, w_hi), (sh_hi, w_lo), (sh_lo, w_hi), (sh_tail, wt_hi),
                                            (sh_rest, wt_lo))):
                    for e in range(GRP):
                        mm = nc.tensor.matmul(psum[:, b0 + e, 0:4 * HID], a[:, par, :], w[:, q * GRP + e, :],
                                              start=(i == 0), stop=(i == 4))
                mm.then_inc(s_hid, 1)

            def turn(t, par, first, last):
                pe.wait_ge(s_g, t * GRPS + GRPS)
                if isinstance(t, int) and t == 0 and first == 0:
                    pe.wait_ge(s_gs, 1)
                else:
                    pe.wait_ge(s_gt, t * 2 + (first > 0))
                for c in range(first, last):
                    n = 128 if c < GC - 1 else GLAST
                    mm = nc.tensor.transpose(psum[0:n, 6, (c % 4) * 128:(c % 4 + 1) * 128],
                                             g[:, par, c * 128:c * 128 + n], id_sb[:, :])
                mm.then_inc(s_gtr, 1)

            def residual(t, par):
                pe.wait_ge(s_ot, CREDIT + t)
                nc.tensor.matmul(psum[:, 7, 0:D0], sh_hi[:, par, :], id_r[:, :], start=True, stop=False,
                                 skip_group_check=True)
                nc.tensor.matmul(psum[:, 7, 0:D0], sh_lo[:, par, :], id_r[:, :], start=False, stop=False,
                                 skip_group_check=True)
                nc.tensor.matmul(psum[:, 7, D0:D], sh_tail[:, par, :], pair_r[:, :], start=False, stop=False,
                                 skip_group_check=True).then_inc(s_resid, 1)

            def experts_out(t):
                pe.wait_ge(s_gt, t * 2 + 2)
                for c in range(GC):
                    n = 128 if c < GC - 1 else GLAST
                    mm = nc.tensor.matmul(psum[:, 7, 0:D], gt[0:n, c, :], w2_sb[0:n, c, :], start=False,
                                          stop=(c == GC - 1), skip_group_check=True)
                mm.then_inc(s_op, 1)

            def tile(t, par):
                pe.wait_ge(s_stage, CREDIT + t + 1)
                hidden(t, par, 0)
                turn(t - 1, 1 - par, 0, 4)
                hidden(t, par, 1)
                residual(t - 1, 1 - par)
                turn(t - 1, 1 - par, 4, GC)
                hidden(t, par, 2)
                experts_out(t - 1)

            pe.wait_ge(s_wlo, 2 * GRPS)
            pe.wait_ge(s_stage, CREDIT + 1)
            for q in range(GRPS):
                hidden(0, 0, q)
            with pe.Fori(0, TILES // 2 - 1) as t2:
                for j in range(2):
                    tile(t2 * 2 + 1 + j, 1 - j)
            tile(TILES - 1, 1)
            turn(TILES - 1, 1, 0, 4)
            residual(TILES - 1, 1)
            turn(TILES - 1, 1, 4, GC)
            experts_out(TILES - 1)

        @block.scalar
        def _(act):
            def fn(out, in_, f, s=None, **kw):
                i = nc.scalar.activation(out, in_, f, **kw)
                return i.then_inc(s, 1) if s is not None else i

            def decay(o, par, m):
                act.wait_ge(s_h, AB_CREDIT + o * PAIRS + m - AB + 1)
                for k in range(3):
                    b = bias_low[:, 2 * m + k:2 * m + k + 1] if k < 2 else bias_high[:, m:m + 1]
                    i = fn(images(abar[:, m % AB, k, :])[:, :, 1:], images(lnd[:, par, k // 2, :])[:, :, 1:],
                           ACT.Tanh, None, scale=-0.5, bias=b)
                i.then_inc(s_a, 1)

            def prepare(x, par, part, behind=True):
                bdt = lambda k: vec[:, V_BDT + k:V_BDT + k + 1]
                if part == 0:
                    act.wait_ge(s_low, x + 1)
                    fn(low[:, :], psum[0:DT_RANK, 6, 0:W], ACT.Copy, s_lows)
                    for k in range(2):
                        act.wait_ge(s_z, x * 2 + k + 1)
                        fn(za[:, k, :], psum[:, 7 - k, 0:W], ACT.Abs, s_sp, bias=bdt(k))
                if part == 1:
                    if behind:
                        act.wait_ge(s_u, x * 3)
                    for k in range(2):
                        fn(zr[:, k, :], psum[:, 7 - k, 0:W], ACT.Relu, s_sp, bias=bdt(k))
                    act.wait_ge(s_sp, x * 6 + 2)
                    fn(ze[:, :, :], za[:, :, :], ACT.Exp, s_sp, scale=-1.0)
                    act.wait_ge(s_sp, x * 6 + 5)
                    fn(dl[:, :, :], ze[:, :, :], ACT.Ln, s_sp, bias=1.0)
                if part == 2:
                    act.wait_ge(s_spv, x + 1)
                    fn(ze[:, :, :], dl[:, :, :], ACT.Square, s_sq)
                    act.wait_ge(s_bc, x + 1)
                    fn(bc1[:, :], psum[0:96, 7, 0:W], ACT.Copy, s_bcact)
                if part == 3:
                    act.wait_ge(s_ms, x + 1)
                    fn(rt[:, :], psum[:, 6, 0:W], ACT.Ln, s_msact, scale=1.0 / D, bias=ms_eps[:, 0:1])
                    act.wait_ge(s_msact, x * 2 + 1)
                    fn(rs[:, :], rt[:, :], ACT.Exp, s_msact, scale=-0.5)
                    act.wait_ge(s_bcsplit, x * 2 + 1)
                    fn(bc2[:, :], bct[:, :], ACT.Copy, s_bcact)
                if part == 4:
                    act.wait_ge(s_rms, x * 5 + 5)
                    fn(za[:, :, :], dl[:, :, :], ACT.Tanh, s_tanh, scale=1.0 / HALF, bias=clamp_bias[:, 0:1])
                    act.wait_ge(s_tanh, x + 1)
                    fn(lnd[:, par, :, :], za[:, :, :], ACT.Ln, s_lnd, scale=HALF, bias=center[:, 0:1])
                    act.wait_ge(s_lnd, x * 2 + 1)
                    fn(ze[:, :, :], lnd[:, par, :, :], ACT.Exp, s_lnd, scale=0.5)

            def split_weights(q):
                act.wait_ge(s_raw, (q + 1) * 48)
                own = slice(q * GRP, (q + 1) * GRP)
                fn(w_hi[:, own, :], raw_low[:, :, :], ACT.Copy)
                fn(wt_hi[:, own, :], raw_tail[:, :, :], ACT.Copy)
                if q:
                    act.wait_ge(s_wlo, q * 2)
                fn(rest_hi[:, :, :], raw_rest[:, :, :], ACT.Identity, s_whi, scale=vec[0:D1 + 2, V_BIAS:V_BIAS + 1])

            def octet(o, par, next_states):
                for m in range(PAIRS):
                    if next_states and m < 5:
                        prepare(o + 1, 1 - par, m)
                    if m + 2 < PAIRS:
                        decay(o, par, m + 2)
                    elif next_states:
                        decay(o + 1, 1 - par, m + 2 - PAIRS)
                    if not next_states and m % 2 == 0 and m // 2 < GRPS:
                        split_weights(m // 2)
                act.wait_ge(s_y, Y_CREDIT + (o + 1) * PAIRS)
                for p, b, dst in ((128, 4, res_low), (D1, 5, res_high)):
                    fn(dst[:, bass.ds(o * TOK, TOK)].rearrange("p (i s) -> p i s", s=PATCHES),
                       images(psum[0:p, b, 0:W])[:, :, 1:], ACT.Copy, s_res)

            act.wait_ge(s_setup, 1)
            for part in range(5):
                prepare(0, 0, part, behind=False)
            for m in range(2):
                decay(0, 0, m)
            with act.Fori(0, LOOPED // 2) as o2:
                for par in range(2):
                    octet(o2 * 2 + par, par, True)
            octet(OCTS - 2, 0, True)
            octet(OCTS - 1, 1, False)

            with act.Fori(0, TILES // 2) as t2:
                for par in range(2):
                    t = t2 * 2 + par
                    act.wait_ge(s_htr, t + 1)
                    fn(h_hi[:, bass.ds(t * 128, 128)], psum[:, 2 + par, 0:128], ACT.Copy)
                    fn(tail_hi[:, par, :], psum[:, 4 + par, 0:128], ACT.Copy, s_hcopy)

            act.wait_ge(s_gs, 3)
            nc.scalar.activation(prob[:, :, :], score[:, :, :], ACT.Exp).then_inc(s_gx, 1)

            def own_h3(t, par, q):
                b0 = (par + q) % 2 * GRP
                act.wait_ge(s_hid, t * GRPS + q + 1)
                fn(h3[:, (par + q) % 2], psum[:, b0:b0 + GRP, 2 * HID:4 * HID], ACT.Copy, s_h3)

            def own_sigmoid(t, par, q):
                act.wait_ge(s_clip, (t * GRPS + q) * 2 + 1)
                fn(sg[:, (par + q) % 2, :], xg[:, (par + q) % 2, :], ACT.Sigmoid, s_sig, scale=1.702)

            def copy_turned(t, part):
                act.wait_ge(s_gtr, CREDIT + t * 2 + part + 1)
                if part == 0:
                    if not (isinstance(t, int) and t == 0):
                        act.wait_ge(s_op, CREDIT + t)
                    fn(gt[:, 0:4, :], psum[:, 6, 0:512].rearrange("p (c n) -> p c n", n=128), ACT.Copy, s_gt)
                else:
                    fn(gt[:, 4:6, :], psum[:, 6, 0:256].rearrange("p (c n) -> p c n", n=128), ACT.Copy)
                    fn(gt[0:GLAST, 6, :], psum[0:GLAST, 6, 256:384], ACT.Copy, s_gt)

            def tile(t, par, before):
                own_h3(t, par, 0)
                if before:
                    copy_turned(t - 1, 0)
                own_sigmoid(t, par, 0)
                own_h3(t, par, 1)
                if before:
                    copy_turned(t - 1, 1)
                own_sigmoid(t, par, 1)
                own_h3(t, par, 2)
                own_sigmoid(t, par, 2)

            tile(0, 0, False)
            with act.Fori(0, TILES // 2 - 1) as t2:
                for j in range(2):
                    tile(t2 * 2 + 1 + j, 1 - j, True)
            tile(TILES - 1, 1, True)
            for part in range(2):
                copy_turned(TILES - 1, part)

        @block.gpsimd
        def _(pool):
            for q in range(GRPS):
                own = slice(q * GRP, (q + 1) * GRP)
                pool.wait_ge(s_whi, q + 1)
                nc.gpsimd.tensor_tensor(w_lo[:, own, :], raw_low[:, :, :], w_hi[:, own, :].bitcast(F32),
                                        ALU.subtract).then_inc(s_wlo, 1)
                nc.gpsimd.tensor_tensor(wt_lo[:, own, :], raw_rest[:, :, :], rest_hi[:, :, :].bitcast(F32),
                                        ALU.subtract).then_inc(s_wlo, 1)
            pool.wait_ge(s_res, CREDIT + OCTS * 2)
            with pool.Fori(0, TILES // 2) as t2:
                for par in range(2):
                    t = t2 * 2 + par
                    pool.wait_ge(s_rtr, CREDIT + t2 * 2)
                    nc.gpsimd.tensor_copy(rl[:, par, :], res_low[:, bass.ds(t * 128, 128)])
                    nc.gpsimd.tensor_copy(rh[:, par, :], res_high[:, bass.ds(t * 128, 128)]).then_inc(s_turn, 1)
                for par in range(2):
                    t = t2 * 2 + par
                    pool.wait_ge(s_ln, t2 * 6 + 5 + par)
                    nc.gpsimd.tensor_tensor(rstd[:, par:par + 1], mv_eps[:, par:par + 1], minus_half[:, 0:1],
                                            ALU.pow).then_inc(s_rstd, 1)

            def stage(t, par):
                cols = bass.ds(t * 128, 128) if not isinstance(t, int) else slice(t * 128, t * 128 + 128)
                nc.gpsimd.tensor_copy(sh_hi[:, par, :], h_hi[:, cols])
                nc.gpsimd.tensor_copy(sh_lo[:, par, :], h_lo[:, cols])
                nc.gpsimd.tensor_copy(sh_rest[0:D1, par, :], h_tail[0:D1, cols])
                nc.gpsimd.tensor_copy(sh_tail[:, par, :], h_tail[:, cols]).then_inc(s_stage, 1)

            def out_rstd(t, par):
                pool.wait_ge(s_ostat, t * 3 + 3)
                nc.gpsimd.tensor_tensor(orstd[:, par:par + 1], oeps[:, par:par + 1], minus_half[:, 0:1],
                                        ALU.pow).then_inc(s_orstd, 1)

            pool.wait_ge(s_hout, CREDIT + TILES)
            pool.wait_ge(s_rest1, 1)
            for t in range(2):
                stage(t, t)
            with pool.Fori(0, TILES // 2 - 1) as t2:
                for j in range(2):
                    t = t2 * 2 + 1 + j
                    pool.wait_ge(s_resid, t)
                    stage(t + 1, j)
                    out_rstd(t - 1, j)
            for t in (TILES - 2, TILES - 1):
                out_rstd(t, t % 2)

        @block.vector
        def _(dve):
            V = nc.vector
            for i, (credited, n) in enumerate(((s_res, CREDIT), (s_hout, CREDIT), (s_stage, CREDIT),
                                               (s_ot, CREDIT), (s_op, CREDIT), (s_gtr, CREDIT), (s_idle, CREDIT),
                                               (s_ch, CREDIT), (s_hn, CREDIT), (s_rtr, CREDIT), (s_h, AB_CREDIT),
                                               (s_y, Y_CREDIT))):
                V.memset(idle[0:1, 2 + i:3 + i], 0.0).then_inc(credited, n)
            V.memset(idle[0:1, 1:2], 0.0).then_inc(s_out, CREDIT_DMA)
            V.memset(ones_sb[:, :], 1.0)
            V.memset(minus_half[:, :], -0.5)
            V.memset(abar[:, :, :, :], 0.0)
            V.memset(xsum[:, :, :], 0.0)
            V.memset(ms_eps[:, :], 1e-6)
            V.memset(center[:, :], CENTER)
            V.memset(clamp_bias[:, :], -CENTER / HALF).then_inc(s_vec, 1)
            dve.wait_ge(s_w1, 16 * N_W1)
            V.tensor_scalar(bias_low[:, :], vec[:, V_ALOW:V_ALOW + STATES], LN2, -0.5, ALU.subtract, ALU.mult)
            V.tensor_scalar(bias_high[:, :], vec[:, V_AHIGH:V_AHIGH + PAIRS], LN2, -0.5, ALU.subtract, ALU.mult)
            V.tensor_scalar(one_plus_d[:, :], vec[:, V_D:V_D + 2], 1.0, None, ALU.add).then_inc(s_vec, 1)
            dve.wait_ge(s_vec, 2)
            for k, p in ((0, 128), (1, D1)):
                V.tensor_scalar(diag_d[0:p, k, 0:p], id_sb[0:p, 0:p], one_plus_d[0:p, k:k + 1], None, ALU.mult)
            for k in range(2):
                V.tensor_scalar(pos_sb[:, k, 1:], pos_sb[:, k, 1:], vec[:, V_TB + k:V_TB + k + 1], None, ALU.add)
            V.tensor_copy(id_r[:, :], id_sb[:, :])
            V.tensor_copy(pair_r[:, :], pair_sb[:, :])
            V.tensor_copy(sel[:, 0:32, :], pick_sb[:, 0:32].unsqueeze(2).to_broadcast([96, 32, 128]))
            V.tensor_copy(sel[:, 32:48, 0:64], pick_sb[:, 0:32:2].unsqueeze(2).to_broadcast([96, 16, 64]))
            V.tensor_copy(sel[:, 32:48, 64:128],
                          pick_sb[:, 1:32:2].unsqueeze(2).to_broadcast([96, 16, 64])).then_inc(s_setup, 1)
            dve.wait_ge(s_setup, 1)

            def f3(t):
                return t.rearrange("p a b -> p (a b)")

            def tokens(x, par, k):
                dve.wait_ge(s_emb, x * 2 + k + 1)
                V.tensor_tensor(images(xt[:, par, k, :]), images(psum[:, 7 - k, 0:W]),
                                pos_sb[:, k, :].unsqueeze(1).to_broadcast([128, OCT, SLOT]), ALU.add).then_inc(s_xt, 1)

            def states(x, par, part):
                if part == 0:
                    dve.wait_ge(s_xt, x * 2 + 2)
                    V.tensor_tensor(f3(xsum[:, :, :])[:, 1:], f3(xt[:, par])[:, 1:], f3(xt[:, par])[:, :2 * W - 1],
                                    ALU.add).then_inc(s_xsum, 1)
                if part == 1:
                    dve.wait_ge(s_sp, x * 6 + 6)
                    V.tensor_tensor(f3(dl[:, :, :]), f3(dl[:, :, :]), f3(zr[:, :, :]), ALU.add).then_inc(s_spv, 1)
                if part == 2:
                    dve.wait_ge(s_bcact, x * 2 + 1)
                    V.scalar_tensor_tensor(out=bct[:, :], in0=bc1[:, :], scalar=pick_sb[:, 32:33],
                                           in1=psum[0:96, 7, 0:W], op0=ALU.mult, op1=ALU.add).then_inc(s_bcsplit, 1)
                if part == 3:
                    dve.wait_ge(s_bcact, x * 2 + 2)
                    V.scalar_tensor_tensor(out=bcs[:, par, :], in0=bc2[:, :], scalar=pick_sb[:, 33:34],
                                           in1=bct[:, :], op0=ALU.mult, op1=ALU.add).then_inc(s_bcsplit, 1)
                    dve.wait_ge(s_msact, x * 2 + 2)
                    V.scalar_tensor_tensor(out=rt[:, :], in0=rs[:, :], scalar=-0.5 / D, in1=rs[:, :],
                                           op0=ALU.mult, op1=ALU.mult).then_inc(s_rms, 1)
                    dve.wait_ge(s_rms, x * 5 + 1)
                    V.scalar_tensor_tensor(out=rt[:, :], in0=psum[:, 6, 0:W], scalar=1e-6 * D, in1=rt[:, :],
                                           op0=ALU.add, op1=ALU.mult).then_inc(s_rms, 1)
                if part == 4:
                    dve.wait_ge(s_rms, x * 5 + 2)
                    V.scalar_tensor_tensor(out=rs[:, :], in0=rt[:, :], scalar=1.5, in1=rs[:, :],
                                           op0=ALU.add, op1=ALU.mult).then_inc(s_rms, 1)
                    dve.wait_ge(s_rms, x * 5 + 3)
                    for k in range(2):
                        V.scalar_tensor_tensor(out=dl[:, k, :], in0=dl[:, k, :],
                                               scalar=vec[:, V_RMS + k:V_RMS + k + 1], in1=rs[:, :],
                                               op0=ALU.mult, op1=ALU.mult).then_inc(s_rms, 1)
                if part == 5:
                    dve.wait_ge(s_lnd, x * 2 + 2)
                    dve.wait_ge(s_xsum, x + 1)
                    for k in range(3):
                        V.scalar_tensor_tensor(out=u[:, par, k, :], in0=xsum[:, k // 2, :], scalar=0.25,
                                               in1=ze[:, k // 2, :], op0=ALU.mult, op1=ALU.mult).then_inc(s_u, 1)

            bank_b = flat[:, 0:3 * W]
            bank_c = flat[:, 1024:1024 + 3 * W]

            def make_v(o, par, m):
                dve.wait_ge(s_b, o * PAIRS + m + 1)
                if m == 0:
                    dve.wait_ge(s_u, (o + 1) * 3)
                V.tensor_tensor(f3(v[:, :, :]), f3(u[:, par]), bank_b, ALU.mult).then_inc(s_v, 1)

            def make_bx(o, m):
                dve.wait_ge(s_a, o * PAIRS + m + 1)
                dve.wait_ge(s_v, o * PAIRS + m + 1)
                V.scalar_tensor_tensor(out=f3(bx[:, :, :]), in0=f3(abar[:, m % AB]), scalar=1.0,
                                       in1=f3(v[:, :, :]), op0=ALU.add, op1=ALU.mult).then_inc(s_bx, 1)

            def octet(o, par, next_states, next_tokens):
                n0 = o * PAIRS
                for m in range(PAIRS):
                    dve.wait_ge(s_bx, n0 + m + 1)
                    V.tensor_tensor_scan(f3(h[:, :, :]), f3(abar[:, m % AB]), f3(bx[:, :, :]), 0.0,
                                         ALU.mult, ALU.add).then_inc(s_h, 1)
                    if m + 1 < PAIRS:
                        make_v(o, par, m + 1)
                    elif next_states:
                        make_v(o + 1, 1 - par, 0)
                    dve.wait_ge(s_h, AB_CREDIT + n0 + m + 1)
                    dve.wait_ge(s_c, n0 + m + 1)
                    dve.wait_ge(s_y, Y_CREDIT + n0 + m - 1)
                    V.tensor_tensor(f3(ch[:, m % 2]), f3(h[:, :, :]), bank_c, ALU.mult).then_inc(s_ch, 1)
                    if m + 1 < PAIRS:
                        make_bx(o, m + 1)
                    elif next_states:
                        make_bx(o + 1, 0)
                    if next_states and m in STATES_AT:
                        states(o + 1, 1 - par, STATES_AT[m])
                    if next_tokens and m >= PAIRS - 2:
                        tokens(o + 2, par, m - PAIRS + 2)

            STATES_AT = {0: 0, 1: 1, 2: 2, 3: 3, 4: 4, 6: 5}

            for k in range(2):
                tokens(0, 0, k)
            for part in range(6):
                states(0, 0, part)
                if part == 4:
                    for k in range(2):
                        tokens(1, 1, k)
            make_v(0, 0, 0)
            make_bx(0, 0)
            with dve.Fori(0, LOOPED // 2) as o2:
                for par in range(2):
                    octet(o2 * 2 + par, par, True, True)
            octet(OCTS - 2, 0, True, False)
            octet(OCTS - 1, 1, False, False)

            for par in range(2):
                V.tensor_copy(sh_rest[D1:D1 + 2, par, :], ones_sb[D1:D1 + 2, :])
            V.memset(comb[:, :, EXPERTS:NE], 1.0).then_inc(s_rest1, 1)
            with dve.Fori(0, TILES // 2) as t2:
                dve.wait_ge(s_rtr, CREDIT + t2 * 2 + 2)
                for par in range(2):
                    V.bn_stats(st6[:, par, :], psum[:, par, 0:D]).then_inc(s_ln, 1)
                dve.wait_ge(s_idle, CREDIT + t2)
                dve.wait_ge(s_ln, t2 * 6 + 2)
                V.memset(idle[0:1, 0:1], 0.0).then_inc(s_idle, 1)
                for par in range(2):
                    V.bn_aggr(mv[:, par, :], st6[:, par, :]).then_inc(s_ln, 1)
                dve.wait_ge(s_ln, t2 * 6 + 4)
                for par in range(2):
                    V.tensor_scalar(mv_eps[:, par:par + 1], mv[:, par, 1:2], 1e-5, None, ALU.add).then_inc(s_ln, 1)
                for par in range(2):
                    dve.wait_ge(s_rstd, t2 * 2 + par + 1)
                    V.tensor_scalar(hn[:, par, 0:D], psum[:, par, 0:D], mv[:, par, 0:1], rstd[:, par:par + 1],
                                    ALU.subtract, ALU.mult)
                    V.tensor_scalar(hn[:, par, D:D + D1], psum[:, par, D0:D], mv[:, par, 0:1], rstd[:, par:par + 1],
                                    ALU.subtract, ALU.mult).then_inc(s_hn, 1)
                for par in range(2):
                    cols = bass.ds((t2 * 2 + par) * 128, 128)
                    dve.wait_ge(s_hcopy, t2 * 2 + par + 1)
                    V.tensor_tensor(h_lo[:, cols], psum[:, 2 + par, 0:128], h_hi[:, cols].bitcast(F32), ALU.subtract)
                    V.scalar_tensor_tensor(out=h_tail[:, cols], in0=tail_hi[:, par, :].bitcast(F32),
                                           scalar=vec[:, V_TAIL:V_TAIL + 1], in1=psum[:, 4 + par, 0:128],
                                           op0=ALU.mult, op1=ALU.add).then_inc(s_hout, 1)

            dve.wait_ge(s_w2, 16 * N_W2)
            for k in range(2):
                V.tensor_copy(gate_r[:, 2 * k, :], gate_w_sb[:, k, :]).then_inc(s_gate, 1)
            dve.wait_ge(s_gate, 2)
            for k in range(2):
                V.tensor_tensor(gate_r[:, 2 * k + 1, :], gate_w_sb[:, k, :], gate_r[:, 2 * k, :].bitcast(F32),
                                ALU.subtract).then_inc(s_gate, 1)
            steps = [0]

            def step(i):
                steps[0] += 1
                i.then_inc(s_gs, 1)
                dve.wait_ge(s_gs, steps[0])

            B3 = [128, TILES, EXPERTS]
            dve.wait_ge(s_gl, 1)
            step(V.tensor_copy(keep8[:, :, :], psum[:, 6, 0:TILES * EXPERTS].rearrange("p (t e) -> p t e", e=EXPERTS)))
            step(V.tensor_reduce(row[:, :], keep8[:, :, :], AX.X, ALU.max))
            step(V.tensor_tensor(score[:, :, :], keep8[:, :, :], row[:, :].unsqueeze(2).to_broadcast(B3), ALU.subtract))
            dve.wait_ge(s_gx, 1)
            step(V.tensor_reduce(row[:, :], prob[:, :, :], AX.X, ALU.add))
            step(V.reciprocal(row[:, :], row[:, :]))
            step(V.tensor_tensor(prob[:, :, :], prob[:, :, :], row[:, :].unsqueeze(2).to_broadcast(B3), ALU.mult))
            step(V.tensor_tensor(score[:, :, :], prob[:, :, :],
                                 gate_b_sb[:, :].unsqueeze(1).to_broadcast(B3), ALU.add))
            step(V.tensor_tensor(g4[:, :, :], score[:, :, 0::2], score[:, :, 1::2], ALU.add))

            def rank(dst, s, n):
                mine = s.unsqueeze(3).to_broadcast([128, TILES, n, n])
                other = s.unsqueeze(2).to_broadcast([128, TILES, n, n])
                a, b = cmpa[:, :, 0:n, 0:n], cmpb[:, :, 0:n, 0:n]
                step(V.tensor_tensor(a, other, mine, ALU.is_equal))
                step(V.tensor_tensor(a, a, below_sb[:, 0:n, 0:n].unsqueeze(1).to_broadcast([128, TILES, n, n]),
                                     ALU.mult))
                step(V.tensor_tensor(b, other, mine, ALU.is_gt))
                step(V.tensor_tensor(a, a, b, ALU.add))
                step(V.tensor_reduce(dst, a, AX.X, ALU.add))

            rank(r4[:, :, :], g4[:, :, :], 4)
            step(V.tensor_scalar(k4[:, :, :], r4[:, :, :], 2.0, None, ALU.is_lt))
            step(V.tensor_scalar(r4[:, :, :], k4[:, :, :], BIG, -BIG, ALU.mult, ALU.add))
            for k in range(2):
                step(V.tensor_tensor(score[:, :, k::2], score[:, :, k::2], r4[:, :, :], ALU.add))
            rank(keep8[:, :, :], score[:, :, :], EXPERTS)
            step(V.tensor_scalar(keep8[:, :, :], keep8[:, :, :], 2.0, None, ALU.is_lt))
            step(V.tensor_tensor(comb[:, :, 0:EXPERTS], keep8[:, :, :], prob[:, :, :], ALU.mult))

            def group(t, par, q):
                n = (par + q) % 2
                b0 = n * GRP
                k = t * GRPS + q
                dve.wait_ge(s_h3, k + 1)
                V.tensor_tensor(prod[:, n].rearrange("p w (e i) -> p e w i", e=GRP),
                                psum[:, b0:b0 + GRP, 0:2 * HID].rearrange("p e (w i) -> p e w i", w=2),
                                h3[:, n].rearrange("p e (w i) -> p e w i", w=2), ALU.mult).then_inc(s_prod, 1)
                dve.wait_ge(s_prod, k + 1)
                V.tensor_scalar(xg[:, n, :], prod[:, n, 0, :], 7.0, None, ALU.min).then_inc(s_clip, 1)
                V.tensor_scalar(xl[:, n, :], prod[:, n, 1, :], -7.0, 7.0, ALU.max, ALU.min).then_inc(s_clip, 1)
                dve.wait_ge(s_clip, k * 2 + 2)
                V.scalar_tensor_tensor(out=xa[:, n, :], in0=xl[:, n, :], scalar=1.0, in1=xg[:, n, :],
                                       op0=ALU.add, op1=ALU.mult).then_inc(s_xa, 1)
                dve.wait_ge(s_xa, k + 1)
                dve.wait_ge(s_sig, k + 1)
                for e in range(GRP):
                    x = q * GRP + e
                    own = slice(e * HID, (e + 1) * HID)
                    i = V.scalar_tensor_tensor(out=g[:, par, x * HID:(x + 1) * HID], in0=xa[:, n, own],
                                               scalar=wt[:, par, x:x + 1], in1=sg[:, n, own],
                                               op0=ALU.mult, op1=ALU.mult)
                i.then_inc(s_g, 1)

            def norm_out(t, par):
                dve.wait_ge(s_op, CREDIT + t + 1)
                V.bn_stats(o6[:, :], psum[:, 7, 0:D]).then_inc(s_ostat, 1)
                dve.wait_ge(s_ostat, t * 3 + 1)
                dve.wait_ge(s_idle, CREDIT + t + TILES // 2)
                V.memset(idle[0:1, 0:1], 0.0).then_inc(s_idle, 1)
                V.bn_aggr(omv[:, par, :], o6[:, :]).then_inc(s_ostat, 1)
                dve.wait_ge(s_ostat, t * 3 + 2)
                V.tensor_scalar(oeps[:, par:par + 1], omv[:, par, 1:2], 1e-5, None, ALU.add).then_inc(s_ostat, 1)
                dve.wait_ge(s_orstd, t + 1)
                dve.wait_ge(s_out, CREDIT_DMA + t * 16)
                V.tensor_scalar(ot[:, par, :], psum[:, 7, 0:D], omv[:, par, 0:1], orstd[:, par:par + 1],
                                ALU.subtract, ALU.mult).then_inc(s_ot, 1)

            def tile(t, par, before):
                cols = bass.ds(t, 1) if not isinstance(t, int) else slice(t, t + 1)
                V.tensor_copy(wt[:, par, :], comb[:, cols, :].rearrange("p o e -> p (o e)")).then_inc(s_wt, 1)
                dve.wait_ge(s_wt, t + 1)
                if before:
                    dve.wait_ge(s_gtr, CREDIT + t * 2 - 2)
                V.tensor_copy(g[:, par, NE * HID:GK], wt[:, par, :])
                for q in range(GRPS):
                    group(t, par, q)
                if before:
                    norm_out(t - 1, 1 - par)

            tile(0, 0, False)
            with dve.Fori(0, TILES // 2 - 1) as t2:
                for j in range(2):
                    tile(t2 * 2 + 1 + j, 1 - j, True)
            tile(TILES - 1, 1, True)
            norm_out(TILES - 1, 1)


def kernel(**inputs):
    import numpy as _np
    import concourse.bacc as _bacc
    from concourse import mybir as _mybir
    from concourse.bass_utils import run_bass_kernel_spmd as _run

    x = {k: _np.asarray(a) for k, a in inputs.items()}

    def padded(a, shape):
        z = _np.zeros(shape, a.dtype)
        z[tuple(slice(0, n) for n in a.shape)] = a
        return z

    def low_high(a, twice=False):
        z = _np.zeros((128, 2, a.shape[1]), a.dtype)
        z[:, 0], z[:D1, 1] = a[:D0], a[D0:]
        if twice:
            z[D1:, 1] = a[D0:]
        return z

    im = x["x"].reshape(OCTS, OCT, 6, 16, 6, 48).transpose(0, 3, 5, 1, 2, 4).reshape(OCTS, KC, 128, OCT, PATCHES)
    patches = _np.zeros((OCTS, 128, KC, OCT, SLOT), im.dtype)
    patches[..., 1:] = im.transpose(0, 2, 1, 3, 4)
    patches = patches.reshape(OCTS, 128, KC, W)
    wt = x["L0_tok_W"].reshape(KC, 128, D).transpose(1, 0, 2)
    w_tok = _np.concatenate([wt, wt[:, :, D0:]], axis=2)
    col = lambda n: low_high(x[n][:, None], True)[:, :, 0]
    a_log = low_high(x["L0_attn_A_log"], True)
    a_high = _np.concatenate([a_log[:D1, 1, 0::2], a_log[:D1, 1, 1::2]], axis=0)
    marks = _np.zeros((128, 2), _np.float32)
    marks[:D1, 0] = marks[D1 + 1, 0] = 1.0
    marks[D1:, 1] = -1.0
    vecs = _np.concatenate([a_log[:, 0], a_high, col("L0_attn_b_dt"), col("L0_attn_rms_scale"),
                            col("L0_attn_D_param"), col("L0_tok_b"), marks], axis=1)
    pos = _np.zeros((128, 2, SLOT), _np.float32)
    pos[:, :, 1:] = low_high(_np.ascontiguousarray(x["L0_tok_pos_emb"].T), True)
    w_bc = low_high(_np.concatenate([x["L0_attn_W_bc"]] * 3, axis=1))
    w_dt = low_high(x["L0_attn_W_dt"])
    w_dtp = _np.concatenate([x["L0_attn_W_dtp"], x["L0_attn_W_dtp"][:, D0:]], axis=1)
    ident = _np.eye(128, dtype=_np.float32)
    pair_ident = _np.concatenate([ident[:D1, :D1]] * 2, axis=0)
    pick = _np.zeros((96, 34), _np.float32)
    pick[:, :32] = _np.concatenate([ident[:32, :32]] * 3, axis=0)
    pick[32:, 32] = -1.0
    pick[64:, 33] = -1.0
    gate_w = low_high(_np.ascontiguousarray(x["L0_ffn_gate_w"].T), True)
    gate_b = _np.ascontiguousarray(_np.broadcast_to(x["L0_ffn_gate_b"], (128, EXPERTS)))
    below = _np.ascontiguousarray(_np.broadcast_to(_np.tri(EXPERTS, EXPERTS, -1, dtype=_np.float32),
                                                   (128, EXPERTS, EXPERTS)))

    def halves(w, ws):
        w = _np.concatenate([w, ws[None]], axis=0)
        return _np.concatenate([w[..., 0::2], w[..., 1::2]], axis=-1)

    w13 = _np.concatenate([halves(x["L0_ffn_W1"], x["L0_ffn_Ws1"]), halves(x["L0_ffn_W3"], x["L0_ffn_Ws3"])], axis=-1)
    b13 = _np.concatenate([halves(x["L0_ffn_B1"], x["L0_ffn_Bs1"]), halves(x["L0_ffn_B3"], x["L0_ffn_Bs3"])], axis=-1)
    groups = lambda a: a.reshape(GRPS, GRP, -1, 4 * HID).transpose(0, 2, 1, 3)
    w13_tail = _np.concatenate([w13[:, D0:]] * 2, axis=1)
    w13_rest = _np.concatenate([w13[:, D0:], b13[:, None], b13[:, None]], axis=1)
    w2 = _np.concatenate([x["L0_ffn_W2"].reshape(-1, D), x["L0_ffn_Ws2"], x["L0_ffn_B2"], x["L0_ffn_Bs2"][None]], axis=0)
    w2 = padded(w2, (GC * 128, D)).reshape(GC, 128, D).transpose(1, 0, 2)
    laid = {"patches": patches, "w_tok": w_tok, "vecs": vecs, "pos": pos, "w_bc": w_bc, "w_dt": w_dt, "w_dtp": w_dtp,
            "ident": ident, "pair_ident": pair_ident, "bc_pick": pick,
            "gate_w": gate_w, "gate_b": gate_b,
            "below": below, "w13_low": groups(w13[:, :D0]), "w13_tail": groups(w13_tail),
            "w13_rest": groups(w13_rest), "w2": w2}

    nc = _bacc.Bacc("TRN2", target_bir_lowering=False, num_devices=1)
    arrays, args = {}, []
    for name, a in laid.items():
        a = _np.ascontiguousarray(a)
        arrays[f"in_{name}_dram"] = a
        args.append(nc.dram_tensor(f"in_{name}_dram", a.shape, _mybir.dt.from_np(a.dtype), kind="ExternalInput").ap())
    out = nc.dram_tensor("out_0_dram", (IMAGES, PATCHES, D), _mybir.dt.float32, kind="ExternalOutput").ap()
    vit_tower(nc, *args, out)
    r = _run(nc, [arrays], core_ids=[0])
    return r.results[0]["out_0_dram"]
```

```python
from contextlib import ExitStack

import concourse.bass as bass
from concourse import mybir

F32 = mybir.dt.float32
F32R = mybir.dt.float32r
ALU = mybir.AluOpType
ACT = mybir.ActivationFunctionType
AX = mybir.AxisListType

IMAGES, PATCHES, D, STATES = 64, 36, 192, 16
D0, D1 = 128, 64
DT_RANK = 48
EXPERTS, HID = 8, 96
SLOT = PATCHES + 1
OCT = 8
OCTS = IMAGES // OCT
W = OCT * SLOT
TOK = OCT * PATCHES
KC = 6
PAIRS = STATES // 2
AB = 8
TILES = IMAGES * PATCHES // 128
BT = 6
BATCHES, BW = TILES // BT, BT * 128
TOKENS = IMAGES * PATCHES
LCH = -(-TOKENS // 512)
NE = EXPERTS + 1
GRP = 3
GRPS = NE // GRP
GK = NE * HID + EXPERTS + 1
GC = -(-GK // 128)
GLAST = GK - (GC - 1) * 128
LO_CLAMP, HI_CLAMP = 0.0001, 10.0
CENTER, HALF = (HI_CLAMP + LO_CLAMP) / 2.0, (HI_CLAMP - LO_CLAMP) / 2.0
LN2 = 0.6931471805599453
BIG = 1e30
LOOPED = OCTS - 2
WARM_UP, WARM_AGAIN = 9, 14
CREDIT, CREDIT_DMA, AB_CREDIT, Y_CREDIT = 1, 16, AB, 2

V_ALOW, V_AHIGH, V_BDT, V_RMS, V_D, V_TB, V_BIAS, V_TAIL, V_N = 0, 16, 24, 26, 28, 30, 32, 33, 34


def vit_tower(nc, patches, w_tok, vecs, pos, w_bc, w_dt, w_dtp, ident, pair_ident, bc_pick,
              gate_w, gate_b, below, w13_low, w13_tail, w13_rest, w2, out):
    with ExitStack() as ctx:
        def sb(name, shape, dt=F32):
            return ctx.enter_context(nc.sbuf_tensor(name, shape, dt))

        def sem(name):
            return ctx.enter_context(nc.semaphore(name))

        psum = ctx.enter_context(nc.psum_tensor("psum", [128, 8, 512], F32))
        patches_v = patches.rearrange("o p c w -> p o c w")
        out_v = out.rearrange("i s n -> (i s) n").rearrange("(t p) n -> p t n", p=128)
        flat = psum[:, :, :].rearrange("p b n -> p (b n)")

        w_tok_sb = sb("w_tok_sb", [128, KC, 256])
        vec = sb("vec", [128, V_N])
        pos_sb = sb("pos_sb", [128, 2, SLOT])
        w_bc_sb = sb("w_bc_sb", [128, 2, 64])
        w_delta = sb("w_delta", [128, 2, 256])
        id_sb = sb("id_sb", [128, 128])
        pair_sb = sb("pair_sb", [128, 64])
        pick_sb = sb("pick_sb", [64, 2 * STATES])
        ones_sb = sb("ones_sb", [128, 128])
        pick = sb("pick", [64, 2 * STATES], F32R)
        pick_two = sb("pick_two", [64, STATES, 128], F32R)
        bias_low = sb("bias_low", [128, STATES])
        bias_high = sb("bias_high", [128, PAIRS])
        one_plus_d = sb("one_plus_d", [128, 2])
        gate_w_sb = sb("gate_w_sb", [128, 2, EXPERTS])
        gate_b_sb = sb("gate_b_sb", [128, EXPERTS])
        below_sb = sb("below_sb", [128, EXPERTS + 1, EXPERTS])
        w_hi = sb("w_hi", [128, NE, 4 * HID], F32R)
        w_lo = sb("w_lo", [128, NE, 4 * HID], F32R)
        wt_hi = sb("wt_hi", [128, NE, 4 * HID], F32R)
        wt_lo = sb("wt_lo", [D1 + 2, NE, 4 * HID], F32R)
        gate_r = sb("gate_r", [128, 4, EXPERTS], F32R)
        ms_eps = sb("ms_eps", [128, 1])
        center = sb("center", [128, 1])
        clamp_bias = sb("clamp_bias", [128, 1])
        idle = sb("idle", [1, 16])
        oeps = sb("oeps", [128, 2])
        minus_half = sb("minus_half", [128, 2])

        res_low = sb("res_low", [128, OCTS * TOK])
        w_dt_sb, w_dtp_sb = res_low[0:DT_RANK, 0:256], res_low[0:DT_RANK, 256:512]
        res_high = sb("res_high", [D1, OCTS * TOK])

        scan_space = ExitStack()

        def scan_sb(name, shape, dt=F32):
            return scan_space.enter_context(nc.sbuf_tensor(name, shape, dt))

        xt = scan_sb("xt", [128, 2, 2, W])
        xsum = scan_sb("xsum", [128, 2, W])
        bcs = scan_sb("bcs", [64, 2, W], F32R)
        zr = scan_sb("zr", [128, 2, W])
        ze = scan_sb("ze", [128, 2, W])
        dl = scan_sb("dl", [128, 2, W])
        rt = scan_sb("rt", [128, W])
        rs = scan_sb("rs", [128, W])
        lnd = scan_sb("lnd", [128, 2, 2, W])
        u = scan_sb("u", [128, 2, 3, W])
        abar = scan_sb("abar", [128, AB, 3, W])
        plus1 = scan_sb("plus1", [128, 2, 3, W])
        v = scan_sb("v", [128, 2, 3, W])
        bx = scan_sb("bx", [128, 2, 3, W])
        h = scan_sb("h", [128, 3, W])
        ch = scan_sb("ch", [128, 2, 3, W])
        diag_d = scan_sb("diag_d", [128, 2, 128])
        patch_space = ExitStack()
        patch_sb = patch_space.enter_context(nc.sbuf_tensor("patch_sb", [128, 2, KC, W], F32))
        patch_space.close()
        raw_low = scan_sb("raw_low", [128, GRP, 4 * HID])
        raw_tail = scan_sb("raw_tail", [128, GRP, 4 * HID])
        raw_rest = scan_sb("raw_rest", [D1 + 2, GRP, 4 * HID])
        rest_hi = scan_sb("rest_hi", [D1 + 2, GRP, 4 * HID], F32R)

        scan_space.close()

        h_hi = sb("h_hi", [128, OCTS * TOK], F32R)
        h_lo = sb("h_lo", [128, OCTS * TOK], F32R)
        h_tail = sb("h_tail", [128, OCTS * TOK], F32R)

        rl = sb("rl", [128, BW])
        rh = sb("rh", [D1, BW])
        st6 = sb("st6", [128, BT, 6])
        mv = sb("mv", [128, BT, 2])
        mv_eps = sb("mv_eps", [128, BT])
        rstd = sb("rstd", [128, BT])
        hn = sb("hn", [128, BT, D + D1])
        tail_hi = sb("tail_hi", [128, BW], F32R)

        w2_sb = sb("w2_sb", [128, GC, D])
        pair_r = sb("pair_r", [128, D1], F32R)
        id_r = sb("id_r", [128, 128], F32R)
        T8 = [128, TILES, EXPERTS]
        prob = sb("prob", T8)
        score = sb("score", T8)
        keep8 = sb("keep8", T8)
        mark = sb("mark", T8)
        cmpa = sb("cmpa", [128, TILES, 4, 4])
        cmpb = sb("cmpb", [128, TILES, 4, 4])
        g4 = sb("g4", [128, TILES, 4])
        r4 = sb("r4", [128, TILES, 4])
        k4 = sb("k4", [128, TILES, 4])
        row = sb("row", [128, TILES])
        last = sb("last", [128, TILES])
        logits = sb("logits", [EXPERTS, TOKENS])
        wt = sb("wt", [128, 2, NE])
        comb = sb("comb", [128, TILES, NE])
        sh_hi = sb("sh_hi", [128, 2, 128], F32R)
        sh_lo = sb("sh_lo", [128, 2, 128], F32R)
        sh_tail = sb("sh_tail", [128, 2, 128], F32R)
        sh_rest = sb("sh_rest", [D1 + 2, 2, 128], F32R)
        h3 = sb("h3", [128, 2, GRP, 2 * HID])
        prod = sb("prod", [128, 2, 2, GRP * HID])
        xg = sb("xg", [128, 2, GRP * HID])
        xl = sb("xl", [128, 2, GRP * HID])
        sg = sb("sg", [128, 2, GRP * HID])
        xa = sb("xa", [128, 2, GRP * HID])
        g = sb("g", [128, 2, GC * 128])
        gt = sb("gt", [128, GC, 128])
        o6 = sb("o6", [128, 6])
        omv = sb("omv", [128, 2, 2])
        orstd = sb("orstd", [128, 2])
        ot = sb("ot", [128, 2, D])

        s_w2b = sem("second_weights_in")
        s_consts = sem("constants_in")
        s_w0, s_w3 = sem("token_first_in"), sem("token_weights_in")
        s_w1, s_w2, s_patch = sem("weights1_in"), sem("weights2_in"), [sem("patch_in0"), sem("patch_in1")]
        s_setup, s_vec = sem("setup_done"), sem("setup_step")
        s_idle = sem("idle_set")
        s_wt = sem("expert_weights_staged")
        s_emb, s_xt = sem("embedded"), sem("xt_ready")
        s_xsum = sem("xsum_ready")
        s_bc, s_bcsplit, s_bcact = sem("bc_product"), sem("bc_split_vec"), sem("bc_split_act")
        s_wd, s_wds = sem("w_delta_product"), sem("w_delta_ready")
        s_z, s_sp, s_spv, s_sq = sem("z_product"), sem("softplus_act"), sem("softplus_vec"), sem("square_ready")
        s_raw, s_whi, s_wlo, s_resid = sem("raw_weights_in"), sem("weights_hi"), sem("weights_lo"), sem("residual_in")
        s_gate, s_lg, s_lgs = sem("gate_weights_split"), sem("logits_product"), sem("logits_copied")
        s_rest1 = sem("ones_rows_set")
        s_hcopy = sem("h_hi_ready")
        s_staged = sem("batch_staged")
        s_ln, s_dup = sem("ln_step"), sem("high_channels_doubled")
        s_ms, s_msact, s_rms = sem("meansq_product"), sem("meansq_act"), sem("rms_vec")
        s_tanh, s_lnd, s_u = sem("clamp_tanh"), sem("log_delta"), sem("u_ready")
        s_a, s_a1, s_b, s_c = sem("abar_ready"), sem("plus1_ready"), sem("b_bcast"), sem("c_bcast")
        s_v, s_bx, s_h, s_ch = sem("v_ready"), sem("bx_ready"), sem("h_ready"), sem("ch_ready")
        s_y = sem("y_added")
        s_res, s_rtr, s_rstd, s_hn = sem("res_ready"), sem("res_turned"), sem("rstd_ready"), sem("hn_ready")
        s_htr, s_hout = sem("hn_turned"), sem("h_stored")
        s_gl, s_gs, s_gx = sem("gate_logits"), sem("gate_step"), sem("gate_exp")
        s_stage, s_hid, s_h3, s_prod = sem("tile_staged"), sem("hidden_ready"), sem("h3_copied"), sem("prod_ready")
        s_clip, s_sig, s_xa, s_g = sem("clipped"), sem("sigmoid_ready"), sem("xa_ready"), sem("g_ready")
        s_gtr, s_gt, s_op = sem("g_turned"), sem("gt_copied"), sem("out_product")
        s_ostat, s_orstd, s_ot, s_out = sem("out_stat"), sem("out_rstd"), sem("out_tile"), sem("out_stored")

        block = ctx.enter_context(nc.Block())

        N_CONSTS, N_W1, N_W2 = 3, 5, 3

        @block.sync
        def _(sp):
            half = KC // 2
            sp.dma_start(w_tok_sb[:, 0:half], w_tok[:, 0:half]).then_inc(s_w0, 16)
            sp.dma_start(patch_sb[:, 0:1, 0:half], patches_v[:, 0:1, 0:half]).then_inc(s_w0, 16)
            sp.dma_start(w_tok_sb[:, half:], w_tok[:, half:]).then_inc(s_w3, 16)
            sp.dma_start(patch_sb[:, 0:1, half:], patches_v[:, 0:1, half:]).then_inc(s_patch[0], 16)
            sp.dma_start(patch_sb[:, 1:2], patches_v[:, 1:2]).then_inc(s_patch[1], 16)
            for dst, src in ((gate_w_sb, gate_w), (gate_b_sb, gate_b), (below_sb, below)):
                sp.dma_start(dst[:], src).then_inc(s_w2, 16)

            def raw_weights(q):
                for dst, src in ((raw_low, w13_low), (raw_tail, w13_tail), (raw_rest, w13_rest)):
                    sp.dma_start(dst[:], src[q]).then_inc(s_raw, 16)

            with sp.Fori(0, OCTS // 2 - 1) as o2:
                for par in range(2):
                    sp.wait_ge(s_emb, (o2 * 2 + par + 1) * 2)
                    sp.dma_start(patch_sb[:, par:par + 1],
                                 patches_v[:, bass.ds(o2 * 2 + 2 + par, 1)]).then_inc(s_patch[par], 16)
            sp.wait_ge(s_emb, OCTS * 2)
            for q in range(GRPS):
                if q:
                    sp.wait_ge(s_wlo, q * 2)
                raw_weights(q)
            sp.wait_ge(s_res, CREDIT + OCTS * 2)
            sp.dma_start(w2_sb[:], w2).then_inc(s_w2b, 16)
            with sp.Fori(0, TILES // 2) as t2:
                for par in range(2):
                    sp.wait_ge(s_ot, CREDIT + t2 * 2 + par + 1)
                    sp.dma_start(out_v[:, bass.ds(t2 * 2 + par, 1), :], ot[:, par:par + 1, :]).then_inc(s_out, 16)
            sp.wait_ge(s_out, CREDIT_DMA + 16 * TILES)

        def images(ap):
            return ap.rearrange("p (i s) -> p i s", s=SLOT)

        @block.tensor
        def _(pe):
            def bank(b, p, n, off=0):
                return psum[0:p, b, off:off + n]

            def embed(x, par, uses, first, last, after=True):
                for i in range(first, last):
                    half, c = i // KC, i % KC
                    if i == (0 if after else KC // 2):
                        pe.wait_ge(s_patch[par], (uses + 1) * 16)
                    if i == 0 and after:
                        pe.wait_ge(s_bcsplit, x)
                    if i == KC and after:
                        pe.wait_ge(s_rms, x * 5 - 3)
                    mm = nc.tensor.matmul(bank(7 - half, 128, W), w_tok_sb[:, c, half * 128:half * 128 + 128],
                                          patch_sb[:, par, c, :], start=(c == 0), stop=(c == KC - 1))
                    if c == KC - 1:
                        mm.then_inc(s_emb, 1)

            def project(x, par, part):
                lo, hi = xt[:, par, 0, :], xt[0:D1, par, 1, :]
                if part == 0:
                    pe.wait_ge(s_xt, (x + 1) * 2)
                    for half in range(2):
                        w = slice(half * 128, half * 128 + 128)
                        nc.tensor.matmul(bank(7 - half, 128, W), w_delta[:, 0, w], lo, start=True, stop=False)
                        nc.tensor.matmul(bank(7 - half, 128, W), w_delta[0:D1, 1, w], hi, start=False,
                                         stop=True).then_inc(s_z, 1)
                if part == 1:
                    pe.wait_ge(s_sp, x * 6 + 4)
                    nc.tensor.matmul(bank(7, 64, W), w_bc_sb[:, 0, :], lo, start=True, stop=False)
                    nc.tensor.matmul(bank(7, 64, W), w_bc_sb[0:D1, 1, :], hi, start=False,
                                     stop=True).then_inc(s_bc, 1)
                if part == 2:
                    pe.wait_ge(s_sq, x + 1)
                    nc.tensor.matmul(bank(6, 128, W), ones_sb[:, :], ze[:, 0, :], start=True, stop=False)
                    nc.tensor.matmul(bank(6, 128, W), ones_sb[0:D1, :], ze[0:D1, 1, :], start=False,
                                     stop=True).then_inc(s_ms, 1)

            def broadcast(m, par, first, b0):
                for seg, c0, c1 in ((0, 0, W), (1, W, 512), (1, 512, 2 * W), (2, 2 * W, 3 * W)):
                    col = first + 2 * m
                    rows = pick[:, col + seg:col + seg + 1].to_broadcast([64, 128]) if seg < 2 else \
                        pick_two[:, col // 2, :]
                    mm = nc.tensor.matmul(flat[:, b0 * 512 + c0:b0 * 512 + c1], rows,
                                          bcs[:, par, c0 - seg * W:c1 - seg * W], start=True, stop=True)
                return mm

            def add_states(o, par, m):
                if m == 0:
                    pe.wait_ge(s_res, CREDIT + o * 2)
                    nc.tensor.matmul(bank(4, 128, W), diag_d[:, 0, :], xt[:, par, 0, :], start=True, stop=False)
                    nc.tensor.matmul(bank(5, 64, W), diag_d[0:D1, 1, 0:D1], xt[0:D1, par, 1, :], start=True,
                                     stop=False)
                pe.wait_ge(s_ch, CREDIT + o * PAIRS + m + 1)
                for k in range(2):
                    nc.tensor.matmul(bank(4, 128, W), id_sb[:, :], ch[:, m % 2, k, :], start=False,
                                     stop=(m == PAIRS - 1 and k == 1))
                nc.tensor.matmul(bank(5, 64, W), pair_sb[:, :], ch[:, m % 2, 2, :], start=False,
                                 stop=(m == PAIRS - 1)).then_inc(s_y, 1)

            def octet(o, par, uses, next_states, next_tokens):
                for m in range(PAIRS):
                    if m + 2 < PAIRS or next_states:
                        pe.wait_ge(s_v, o * PAIRS + m + 2)
                        if m + 2 == PAIRS:
                            pe.wait_ge(s_bcsplit, o + 2)
                        broadcast((m + 2) % PAIRS, (par + (m + 2) // PAIRS) % 2, 0, 0).then_inc(s_b, 1)
                    pe.wait_ge(s_ch, CREDIT + o * PAIRS + m)
                    broadcast(m, par, 16, 2).then_inc(s_c, 1)
                    if next_states and m in PROJECT_A:
                        project(o + 1, 1 - par, PROJECT_A[m])
                    if next_tokens and m in EMBED_A:
                        embed(o + 2, par, uses + 1, *EMBED_A[m])
                    if m:
                        add_states(o, par, m - 1)
                    if next_states and m in PROJECT_B:
                        project(o + 1, 1 - par, PROJECT_B[m])
                    if next_tokens and m in EMBED_B:
                        embed(o + 2, par, uses + 1, *EMBED_B[m])
                    if next_tokens and m == PAIRS - 1:
                        project(o + 2, par, 0)
                add_states(o, par, PAIRS - 1)

            PROJECT_A, PROJECT_B = {1: 1}, {2: 2}
            EMBED_A = {3: (0, 2), 4: (3, 5), 5: (6, 8), 6: (9, 11)}
            EMBED_B = {3: (2, 3), 4: (5, 6), 5: (8, 9), 6: (11, 12)}

            def warm(n):
                for _ in range(n):
                    nc.tensor.matmul(bank(5, 128, 128), ones_sb[:, :], ones_sb[:, :], start=True, stop=True)

            pe.wait_ge(s_vec, 1)
            warm(WARM_UP)
            pe.wait_ge(s_w0, 32)
            embed(0, 0, 0, 0, KC // 2, after=False)
            pe.wait_ge(s_w3, 16)
            embed(0, 0, 0, KC // 2, 2 * KC, after=False)
            pe.wait_ge(s_w1, 16 * N_W1)
            pe.wait_ge(s_setup, 1)
            for half, p in ((0, 128), (1, D1)):
                nc.tensor.matmul(bank(half, p, 256), w_dt_sb[:, half * 128:half * 128 + p], w_dtp_sb[:, :],
                                 start=True, stop=True).then_inc(s_wd, 1)
            pe.wait_ge(s_wds, 2)
            for part in range(3):
                project(0, 0, part)
            embed(1, 1, 0, 0, 2 * KC)
            pe.wait_ge(s_bcsplit, 1)
            broadcast(0, 0, 0, 0).then_inc(s_b, 1)
            project(1, 1, 0)
            warm(WARM_AGAIN)
            pe.wait_ge(s_v, 1)
            broadcast(1, 0, 0, 0).then_inc(s_b, 1)
            with pe.Fori(0, LOOPED // 2) as o2:
                for par in range(2):
                    octet(o2 * 2 + par, par, o2, True, True)
            octet(OCTS - 2, 0, OCTS // 2 - 1, True, False)
            octet(OCTS - 1, 1, OCTS // 2 - 1, False, False)

            def to_tokens(j, i):
                pe.wait_ge(s_staged, j * 2 + 2)
                for k in range(2):
                    cols, off = slice((2 * i + k) * 128, (2 * i + k + 1) * 128), k * D
                    nc.tensor.transpose(psum[:, i, off:off + D0], rl[:, cols], id_sb[:, :])
                    mm = nc.tensor.transpose(psum[:, i, off + D0:off + D], rh[:, cols], id_sb[0:D1, 0:D1])
                mm.then_inc(s_rtr, 1)

            def low_to_channels(j, i):
                pe.wait_ge(s_hn, j * BT + 2 * i + 2)
                for k in (2 * i, 2 * i + 1):
                    mm = nc.tensor.transpose(psum[:, 3 + k // 4, k % 4 * 128:(k % 4 + 1) * 128], hn[:, k, 0:D0],
                                             id_sb[:, :])
                return mm

            def high_to_channels(j):
                pe.wait_ge(s_dup, j + 1)
                for i in range(BT):
                    mm = nc.tensor.transpose(psum[:, 5 + i // 4, i % 4 * 128:(i % 4 + 1) * 128], hn[:, i, D0:D + D1],
                                             id_sb[:, :])
                mm.then_inc(s_htr, 1)

            for i in range(BT // 2):
                to_tokens(0, i)
            with pe.Fori(0, BATCHES - 1) as j:
                pe.wait_ge(s_hout, CREDIT + j * 2)
                for i in range(BT // 2):
                    mm = low_to_channels(j, i)
                    if i == BT // 2 - 1:
                        mm.then_inc(s_htr, 1)
                    to_tokens(j + 1, i)
                high_to_channels(j)
            pe.wait_ge(s_hout, CREDIT + (BATCHES - 1) * 2)
            for i in range(BT // 2):
                mm = low_to_channels(BATCHES - 1, i)
            mm.then_inc(s_htr, 1)
            high_to_channels(BATCHES - 1)

            def logits_product(c):
                cols = slice(c * 512, min((c + 1) * 512, TOKENS))
                for i, (part, w) in enumerate(((h_hi, 0), (h_hi, 1), (h_lo, 0), (h_tail, 2), (h_tail, 3))):
                    mm = nc.tensor.matmul(psum[0:EXPERTS, c, 0:cols.stop - cols.start], gate_r[:, w, :],
                                          part[:, cols], start=(i == 0), stop=(i == 4))
                mm.then_inc(s_lg, 1)

            def logits_turned(c):
                pe.wait_ge(s_lgs, c + 1)
                for t in range(c * 4, min(c * 4 + 4, TILES)):
                    mm = nc.tensor.transpose(psum[:, 7, t * EXPERTS:(t + 1) * EXPERTS],
                                             logits[:, t * 128:(t + 1) * 128], id_sb[0:EXPERTS, 0:EXPERTS])
                return mm

            pe.wait_ge(s_gate, 4)
            for c in range(LCH):
                if c == (TILES - BT) // 4:
                    pe.wait_ge(s_hout, CREDIT + 2 * BATCHES)
                logits_product(c)
                if c:
                    logits_turned(c - 1)
            logits_turned(LCH - 1).then_inc(s_gl, 1)

            def hidden(t, par, q):
                b0 = (par + q) % 2 * GRP
                if not (isinstance(t, int) and t * GRPS + q < 2):
                    pe.wait_ge(s_prod, t * GRPS + q - 1)
                for i, (a, w) in enumerate(((sh_hi, w_hi), (sh_hi, w_lo), (sh_lo, w_hi), (sh_tail, wt_hi),
                                            (sh_rest, wt_lo))):
                    for e in range(GRP):
                        mm = nc.tensor.matmul(psum[:, b0 + e, 0:4 * HID], a[:, par, :], w[:, q * GRP + e, :],
                                              start=(i == 0), stop=(i == 4))
                mm.then_inc(s_hid, 1)

            def turn(t, par, first, last):
                pe.wait_ge(s_g, t * GRPS + GRPS)
                if not (isinstance(t, int) and t == 0 and first == 0):
                    pe.wait_ge(s_gt, t * 2 + (first > 0))
                for c in range(first, last):
                    n = 128 if c < GC - 1 else GLAST
                    mm = nc.tensor.transpose(psum[0:n, 6, (c % 4) * 128:(c % 4 + 1) * 128],
                                             g[:, par, c * 128:c * 128 + n], id_sb[:, :])
                mm.then_inc(s_gtr, 1)

            def residual(t, par):
                pe.wait_ge(s_ot, CREDIT + t)
                nc.tensor.matmul(psum[:, 7, 0:D0], sh_hi[:, par, :], id_r[:, :], start=True, stop=False,
                                 skip_group_check=True)
                nc.tensor.matmul(psum[:, 7, 0:D0], sh_lo[:, par, :], id_r[:, :], start=False, stop=False,
                                 skip_group_check=True)
                nc.tensor.matmul(psum[:, 7, D0:D], sh_tail[:, par, :], pair_r[:, :], start=False, stop=False,
                                 skip_group_check=True).then_inc(s_resid, 1)

            def experts_out(t):
                pe.wait_ge(s_gt, t * 2 + 2)
                for c in range(GC):
                    n = 128 if c < GC - 1 else GLAST
                    mm = nc.tensor.matmul(psum[:, 7, 0:D], gt[0:n, c, :], w2_sb[0:n, c, :], start=False,
                                          stop=(c == GC - 1), skip_group_check=True)
                mm.then_inc(s_op, 1)

            def tile(t, par):
                pe.wait_ge(s_stage, CREDIT + t + 1)
                hidden(t, par, 0)
                turn(t - 1, 1 - par, 0, 4)
                hidden(t, par, 1)
                residual(t - 1, 1 - par)
                turn(t - 1, 1 - par, 4, GC)
                hidden(t, par, 2)
                experts_out(t - 1)

            pe.wait_ge(s_wlo, 2 * GRPS)
            pe.wait_ge(s_w2b, 16)
            pe.wait_ge(s_stage, CREDIT + 1)
            for q in range(GRPS):
                hidden(0, 0, q)
            with pe.Fori(0, TILES // 2 - 1) as t2:
                for j in range(2):
                    tile(t2 * 2 + 1 + j, 1 - j)
            tile(TILES - 1, 1)
            turn(TILES - 1, 1, 0, 4)
            residual(TILES - 1, 1)
            turn(TILES - 1, 1, 4, GC)
            experts_out(TILES - 1)

        @block.scalar
        def _(act):
            def fn(out, in_, f, s=None, **kw):
                i = nc.scalar.activation(out, in_, f, **kw)
                return i.then_inc(s, 1) if s is not None else i

            def decay(o, par, m):
                act.wait_ge(s_h, AB_CREDIT + o * PAIRS + m - AB + 1)
                for k in range(3):
                    b = bias_low[:, 2 * m + k:2 * m + k + 1] if k < 2 else bias_high[:, m:m + 1]
                    i = fn(images(abar[:, m % AB, k, :])[:, :, 1:], images(lnd[:, par, k // 2, :])[:, :, 1:],
                           ACT.Tanh, None, scale=-0.5, bias=b)
                i.then_inc(s_a, 1)

            def plus_one(o, m):
                act.wait_ge(s_a, o * PAIRS + m + 1)
                if not (isinstance(o, int) and o * PAIRS + m < 2):
                    act.wait_ge(s_bx, o * PAIRS + m - 1)
                fn(plus1[:, m % 2], abar[:, m % AB], ACT.Identity, s_a1, bias=1.0)

            def next_plus(o, m, next_states):
                if m + 2 < PAIRS:
                    plus_one(o, m + 2)
                elif next_states:
                    plus_one(o + 1, m + 2 - PAIRS)

            def prepare(x, par, part, behind=True):
                bdt = lambda k: vec[:, V_BDT + k:V_BDT + k + 1]
                if part == 0:
                    if behind:
                        act.wait_ge(s_u, x * 2)
                    for k in range(2):
                        act.wait_ge(s_z, x * 2 + k + 1)
                        fn(ze[:, k, :], psum[:, 7 - k, 0:W], ACT.Abs, s_sp, bias=bdt(k))
                    for k in range(2):
                        fn(zr[:, k, :], psum[:, 7 - k, 0:W], ACT.Relu, s_sp, bias=bdt(k))
                    act.wait_ge(s_sp, x * 6 + 2)
                    fn(ze[:, :, :], ze[:, :, :], ACT.Exp, s_sp, scale=-1.0)
                if part == 1:
                    act.wait_ge(s_sp, x * 6 + 5)
                    fn(dl[:, :, :], ze[:, :, :], ACT.Ln, s_sp, bias=1.0)
                if part == 2:
                    act.wait_ge(s_spv, x + 1)
                    fn(ze[:, :, :], dl[:, :, :], ACT.Square, s_sq)
                    act.wait_ge(s_bc, x + 1)
                    fn(bcs[:, par, :], psum[0:64, 7, 0:W], ACT.Copy, s_bcact)
                if part == 3:
                    act.wait_ge(s_ms, x + 1)
                    fn(rt[:, :], psum[:, 6, 0:W], ACT.Ln, s_msact, scale=1.0 / D, bias=ms_eps[:, 0:1])
                    act.wait_ge(s_msact, x * 2 + 1)
                    fn(rs[:, :], rt[:, :], ACT.Exp, s_msact, scale=-0.5)
                if part == 4:
                    act.wait_ge(s_rms, x * 5 + 5)
                    fn(zr[:, :, :], dl[:, :, :], ACT.Tanh, s_tanh, scale=1.0 / HALF, bias=clamp_bias[:, 0:1])
                    act.wait_ge(s_tanh, x + 1)
                    fn(lnd[:, par, :, :], zr[:, :, :], ACT.Ln, s_lnd, scale=HALF, bias=center[:, 0:1])
                    act.wait_ge(s_lnd, x * 2 + 1)
                    fn(ze[:, :, :], lnd[:, par, :, :], ACT.Exp, s_lnd, scale=0.5)

            def split_weights(q):
                act.wait_ge(s_raw, (q + 1) * 48)
                own = slice(q * GRP, (q + 1) * GRP)
                fn(w_hi[:, own, :], raw_low[:, :, :], ACT.Copy)
                fn(wt_hi[:, own, :], raw_tail[:, :, :], ACT.Copy)
                if q:
                    act.wait_ge(s_wlo, q * 2)
                fn(rest_hi[:, :, :], raw_rest[:, :, :], ACT.Identity, s_whi, scale=vec[0:D1 + 2, V_BIAS:V_BIAS + 1])

            def octet(o, par, next_states, splits={}):
                for m in range(PAIRS):
                    if next_states:
                        for part in PREPARE_AT.get(m, ()):
                            prepare(o + 1, 1 - par, part)
                    if m in PLUS_FIRST:
                        next_plus(o, m, next_states)
                    for k in DECAYS_AT[m]:
                        if k < PAIRS:
                            decay(o, par, k)
                        elif next_states:
                            decay(o + 1, 1 - par, k - PAIRS)
                    if m not in PLUS_FIRST:
                        next_plus(o, m, next_states)
                    if m in splits:
                        split_weights(splits[m])
                act.wait_ge(s_y, Y_CREDIT + (o + 1) * PAIRS)
                for p, b, dst in ((128, 4, res_low), (D1, 5, res_high)):
                    fn(dst[:, bass.ds(o * TOK, TOK)].rearrange("p (i s) -> p i s", s=PATCHES),
                       images(psum[0:p, b, 0:W])[:, :, 1:], ACT.Copy, s_res)

            PREPARE_AT = {0: (0,), 1: (1,), 2: (2, 3), 4: (4,)}
            PLUS_FIRST = (5, 6, 7)
            DECAYS_AT = {0: (5,), 1: (), 2: (6,), 3: (7,), 4: (), 5: (8,), 6: (9, 10), 7: (11, 12)}
            for dst, src in ((vec, vecs), (pos_sb, pos), (pick_sb, bc_pick)):
                act.dma_start(dst[:], src).then_inc(s_consts, 16)
            for dst, src in ((w_dt_sb, w_dt), (w_dtp_sb, w_dtp), (id_sb, ident), (w_bc_sb, w_bc),
                             (pair_sb, pair_ident)):
                act.dma_start(dst[:], src).then_inc(s_w1, 16)
            act.wait_ge(s_setup, 1)
            for part in range(5):
                prepare(0, 0, part, behind=False)
            for m in range(2):
                decay(0, 0, m)
                plus_one(0, m)
            for m in range(2, 5):
                decay(0, 0, m)
            with act.Fori(0, LOOPED // 2) as o2:
                for par in range(2):
                    octet(o2 * 2 + par, par, True)
            octet(OCTS - 2, 0, True, {5: 0})
            octet(OCTS - 1, 1, False, {2: 1})

            def stage_batch(j):
                for dst, src in ((rl, res_low), (rh, res_high)):
                    fn(dst[:, :], src[:, bass.ds(j * BW, BW)] if not isinstance(j, int) else src[:, 0:BW],
                       ACT.Copy, s_staged)

            def leading(j):
                cols = bass.ds(j * BW, BW) if not isinstance(j, int) else slice(j * BW, (j + 1) * BW)
                act.wait_ge(s_htr, j * 2 + 1)
                fn(h_hi[:, cols], flat[:, 3 * 512:3 * 512 + BW], ACT.Copy, s_hcopy)
                act.wait_ge(s_htr, j * 2 + 2)
                fn(tail_hi[:, :], flat[:, 5 * 512:5 * 512 + BW], ACT.Copy, s_hcopy)

            act.wait_ge(s_res, CREDIT + OCTS * 2)
            stage_batch(0)
            split_weights(2)
            with act.Fori(0, BATCHES - 1) as j:
                act.wait_ge(s_rtr, CREDIT + (j + 1) * (BT // 2))
                stage_batch(j + 1)
                leading(j)
            leading(BATCHES - 1)

            for c in range(LCH):
                cols = slice(c * 512, min((c + 1) * 512, TOKENS))
                act.wait_ge(s_lg, c + 1)
                fn(logits[:, cols], psum[0:EXPERTS, c, 0:cols.stop - cols.start], ACT.Copy, s_lgs)
            act.wait_ge(s_gs, 2)
            nc.scalar.activation(prob[:, :, :], score[:, :, :], ACT.Exp).then_inc(s_gx, 1)

            def own_h3(t, par, q):
                b0 = (par + q) % 2 * GRP
                act.wait_ge(s_hid, t * GRPS + q + 1)
                fn(h3[:, (par + q) % 2], psum[:, b0:b0 + GRP, 2 * HID:4 * HID], ACT.Copy, s_h3)

            def own_sigmoid(t, par, q):
                act.wait_ge(s_clip, (t * GRPS + q) * 2 + 1)
                fn(sg[:, (par + q) % 2, :], xg[:, (par + q) % 2, :], ACT.Sigmoid, s_sig, scale=1.702)

            def copy_turned(t, part):
                act.wait_ge(s_gtr, CREDIT + t * 2 + part + 1)
                if part == 0:
                    if not (isinstance(t, int) and t == 0):
                        act.wait_ge(s_op, CREDIT + t)
                    fn(gt[:, 0:4, :], psum[:, 6, 0:512].rearrange("p (c n) -> p c n", n=128), ACT.Copy, s_gt)
                else:
                    fn(gt[:, 4:6, :], psum[:, 6, 0:256].rearrange("p (c n) -> p c n", n=128), ACT.Copy)
                    fn(gt[0:GLAST, 6, :], psum[0:GLAST, 6, 256:384], ACT.Copy, s_gt)

            def tile(t, par, before):
                own_h3(t, par, 0)
                if before:
                    copy_turned(t - 1, 0)
                own_sigmoid(t, par, 0)
                own_h3(t, par, 1)
                if before:
                    copy_turned(t - 1, 1)
                own_sigmoid(t, par, 1)
                own_h3(t, par, 2)
                own_sigmoid(t, par, 2)

            tile(0, 0, False)
            with act.Fori(0, TILES // 2 - 1) as t2:
                for j in range(2):
                    tile(t2 * 2 + 1 + j, 1 - j, True)
            tile(TILES - 1, 1, True)
            for part in range(2):
                copy_turned(TILES - 1, part)

        @block.gpsimd
        def _(pool):
            def input_product(o, m):
                n = o * PAIRS + m
                pool.wait_ge(s_v, n + 1)
                pool.wait_ge(s_a1, n + 1)
                pool.wait_ge(s_h, AB_CREDIT + n - 1)
                nc.gpsimd.tensor_tensor(bx[:, m % 2], plus1[:, m % 2], v[:, m % 2], ALU.mult).then_inc(s_bx, 1)

            def weights_rest(i):
                q = i // 2
                own = slice(q * GRP, (q + 1) * GRP)
                pool.wait_ge(s_whi, q + 1)
                if i % 2 == 0:
                    nc.gpsimd.tensor_tensor(w_lo[:, own, :], raw_low[:, :, :], w_hi[:, own, :].bitcast(F32),
                                            ALU.subtract).then_inc(s_wlo, 1)
                else:
                    nc.gpsimd.tensor_tensor(wt_lo[:, own, :], raw_rest[:, :, :], rest_hi[:, :, :].bitcast(F32),
                                            ALU.subtract).then_inc(s_wlo, 1)

            def token_sum(x, par, behind=True):
                pool.wait_ge(s_xt, (x + 1) * 2)
                if behind:
                    pool.wait_ge(s_u, x * 2)
                nc.gpsimd.tensor_tensor(xsum.rearrange("p k w -> p (k w)")[:, 1:],
                                        xt[:, par].rearrange("p k w -> p (k w)")[:, 1:],
                                        xt[:, par].rearrange("p k w -> p (k w)")[:, :2 * W - 1],
                                        ALU.add).then_inc(s_xsum, 1)

            def scaled_sum(x, par):
                pool.wait_ge(s_lnd, x * 2 + 2)
                pool.wait_ge(s_xsum, x + 1)
                for first, k, n in ((0, 0, 2), (2, 1, 1)):
                    nc.gpsimd.tensor_tensor(u[:, par, first:first + n, :],
                                            xsum[:, k, :].unsqueeze(1).to_broadcast([128, n, W]),
                                            ze[:, k, :].unsqueeze(1).to_broadcast([128, n, W]),
                                            ALU.mult).then_inc(s_u, 1)

            def octet(o, par, next_states, rests={}):
                for m in range(PAIRS):
                    if next_states and m == 5:
                        scaled_sum(o + 1, 1 - par)
                    if m + 1 < PAIRS:
                        input_product(o, m + 1)
                    elif next_states:
                        input_product(o + 1, 0)
                    if next_states and m == 0:
                        token_sum(o + 1, 1 - par)
                    if m in rests:
                        weights_rest(rests[m])

            pool.wait_ge(s_setup, 1)
            token_sum(0, 0, behind=False)
            scaled_sum(0, 0)
            input_product(0, 0)
            with pool.Fori(0, LOOPED // 2) as o2:
                for par in range(2):
                    octet(o2 * 2 + par, par, True)
            octet(OCTS - 2, 0, True, {6: 0, 7: 1})
            octet(OCTS - 1, 1, False, {2: 2, 4: 3})

            def batch_rstd(j):
                pool.wait_ge(s_ln, (j + 1) * (2 * BT + 1))
                nc.gpsimd.tensor_tensor(rstd[:, :], mv_eps[:, :], minus_half[:, 0:1].to_broadcast([128, BT]),
                                        ALU.pow).then_inc(s_rstd, 1)

            batch_rstd(0)
            for i in (4, 5):
                weights_rest(i)
            with pool.Fori(1, BATCHES) as j:
                batch_rstd(j)

            def stage(t, par):
                cols = bass.ds(t * 128, 128) if not isinstance(t, int) else slice(t * 128, t * 128 + 128)
                nc.gpsimd.tensor_copy(sh_hi[:, par, :], h_hi[:, cols])
                nc.gpsimd.tensor_copy(sh_lo[:, par, :], h_lo[:, cols])
                nc.gpsimd.tensor_copy(sh_rest[0:D1, par, :], h_tail[0:D1, cols])
                nc.gpsimd.tensor_copy(sh_tail[:, par, :], h_tail[:, cols]).then_inc(s_stage, 1)

            def out_rstd(t, par):
                pool.wait_ge(s_ostat, t * 3 + 3)
                nc.gpsimd.tensor_tensor(orstd[:, par:par + 1], oeps[:, par:par + 1], minus_half[:, 0:1],
                                        ALU.pow).then_inc(s_orstd, 1)

            pool.wait_ge(s_hout, CREDIT + 2 * BATCHES)
            pool.wait_ge(s_rest1, 1)
            for t in range(2):
                stage(t, t)
            with pool.Fori(0, TILES // 2 - 1) as t2:
                for j in range(2):
                    t = t2 * 2 + 1 + j
                    pool.wait_ge(s_resid, t)
                    stage(t + 1, j)
                    out_rstd(t - 1, j)
            for t in (TILES - 2, TILES - 1):
                out_rstd(t, t % 2)

        @block.vector
        def _(dve):
            V = nc.vector
            for i, (credited, n) in enumerate(((s_res, CREDIT), (s_hout, CREDIT), (s_stage, CREDIT),
                                               (s_ot, CREDIT), (s_op, CREDIT), (s_gtr, CREDIT), (s_idle, CREDIT),
                                               (s_ch, CREDIT), (s_rtr, CREDIT), (s_h, AB_CREDIT),
                                               (s_y, Y_CREDIT))):
                V.memset(idle[0:1, 2 + i:3 + i], 0.0).then_inc(credited, n)
            V.memset(idle[0:1, 1:2], 0.0).then_inc(s_out, CREDIT_DMA)
            V.memset(ones_sb[:, :], 1.0)
            V.memset(minus_half[:, :], -0.5)
            V.memset(abar.rearrange("p b k (i s) -> p (b k i) s", s=SLOT)[:, :, 0:1], 0.0)
            V.memset(xsum[:, 0, 0:1], 0.0)
            V.memset(ms_eps[:, :], 1e-6)
            V.memset(center[:, :], CENTER)
            V.memset(clamp_bias[:, :], -CENTER / HALF).then_inc(s_vec, 1)
            dve.wait_ge(s_consts, 16 * N_CONSTS)
            V.tensor_scalar(bias_low[:, :], vec[:, V_ALOW:V_ALOW + STATES], LN2, -0.5, ALU.subtract, ALU.mult)
            V.tensor_scalar(bias_high[:, :], vec[:, V_AHIGH:V_AHIGH + PAIRS], LN2, -0.5, ALU.subtract, ALU.mult)
            V.tensor_scalar(one_plus_d[:, :], vec[:, V_D:V_D + 2], 1.0, None, ALU.add).then_inc(s_vec, 1)
            dve.wait_ge(s_vec, 2)
            V.tensor_copy(pick[:, :], pick_sb[:, :])
            for k in range(2):
                V.tensor_copy(pick_two[:, :, k * 64:(k + 1) * 64],
                              pick_sb[:, k::2].unsqueeze(2).to_broadcast([64, STATES, 64]))
            for k in range(2):
                i = V.tensor_scalar(pos_sb[:, k, 1:], pos_sb[:, k, 1:], vec[:, V_TB + k:V_TB + k + 1], None, ALU.add)
            i.then_inc(s_setup, 1)
            dve.wait_ge(s_setup, 1)

            def f3(t):
                return t.rearrange("p a b -> p (a b)")

            def tokens(x, par, k):
                dve.wait_ge(s_emb, x * 2 + k + 1)
                V.tensor_tensor(images(xt[:, par, k, :]), images(psum[:, 7 - k, 0:W]),
                                pos_sb[:, k, :].unsqueeze(1).to_broadcast([128, OCT, SLOT]), ALU.add).then_inc(s_xt, 1)

            def states(x, par, part):
                if part == 0:
                    dve.wait_ge(s_sp, x * 6 + 6)
                    V.tensor_tensor(f3(dl[:, :, :]), f3(dl[:, :, :]), f3(zr[:, :, :]), ALU.add).then_inc(s_spv, 1)
                if part == 1:
                    dve.wait_ge(s_bcact, x + 1)
                    V.tensor_tensor(bcs[32:64, par, :], psum[32:64, 7, 0:W], bcs[32:64, par, :].bitcast(F32),
                                    ALU.subtract).then_inc(s_bcsplit, 1)
                if part == 2:
                    dve.wait_ge(s_msact, x * 2 + 2)
                    V.scalar_tensor_tensor(out=rt[:, :], in0=rs[:, :], scalar=-0.5 / D, in1=rs[:, :],
                                           op0=ALU.mult, op1=ALU.mult).then_inc(s_rms, 1)
                    dve.wait_ge(s_rms, x * 5 + 1)
                    V.scalar_tensor_tensor(out=rt[:, :], in0=psum[:, 6, 0:W], scalar=1e-6 * D, in1=rt[:, :],
                                           op0=ALU.add, op1=ALU.mult).then_inc(s_rms, 1)
                if part == 3:
                    dve.wait_ge(s_rms, x * 5 + 2)
                    V.scalar_tensor_tensor(out=rs[:, :], in0=rt[:, :], scalar=1.5, in1=rs[:, :],
                                           op0=ALU.add, op1=ALU.mult).then_inc(s_rms, 1)
                    dve.wait_ge(s_rms, x * 5 + 3)
                    for k in range(2):
                        V.scalar_tensor_tensor(out=dl[:, k, :], in0=dl[:, k, :],
                                               scalar=vec[:, V_RMS + k:V_RMS + k + 1], in1=rs[:, :],
                                               op0=ALU.mult, op1=ALU.mult).then_inc(s_rms, 1)

            bank_b = flat[:, 0:3 * W]
            bank_c = flat[:, 1024:1024 + 3 * W]

            def make_v(o, par, m):
                dve.wait_ge(s_b, o * PAIRS + m + 1)
                if m == 0:
                    dve.wait_ge(s_u, (o + 1) * 2)
                if not (isinstance(o, int) and o * PAIRS + m < 2):
                    dve.wait_ge(s_bx, o * PAIRS + m - 1)
                V.tensor_tensor(f3(v[:, m % 2]), f3(u[:, par]), bank_b, ALU.mult).then_inc(s_v, 1)

            def octet(o, par, next_states, next_tokens):
                n0 = o * PAIRS
                for m in range(PAIRS):
                    dve.wait_ge(s_bx, n0 + m + 1)
                    dve.wait_ge(s_ch, CREDIT + n0 + m)
                    V.tensor_tensor_scan(f3(h[:, :, :]), f3(abar[:, m % AB]), f3(bx[:, m % 2]), 0.0,
                                         ALU.mult, ALU.add).then_inc(s_h, 1)
                    if m + 2 < PAIRS:
                        make_v(o, par, m + 2)
                    elif next_states:
                        make_v(o + 1, 1 - par, m + 2 - PAIRS)
                    dve.wait_ge(s_h, AB_CREDIT + n0 + m + 1)
                    dve.wait_ge(s_c, n0 + m + 1)
                    dve.wait_ge(s_y, Y_CREDIT + n0 + m - 1)
                    V.tensor_tensor(f3(ch[:, m % 2]), f3(h[:, :, :]), bank_c, ALU.mult).then_inc(s_ch, 1)
                    if next_states:
                        for part in STATES_AT.get(m, ()):
                            states(o + 1, 1 - par, part)
                    if next_tokens and m in TOKENS_AT:
                        tokens(o + 2, par, TOKENS_AT[m])

            STATES_AT = {1: (0,), 2: (1,), 3: (2, 3)}
            TOKENS_AT = {5: 0, 6: 1}

            for k in range(2):
                tokens(0, 0, k)
            dve.wait_ge(s_w1, 16 * N_W1)
            for k, p in ((0, 128), (1, D1)):
                V.tensor_scalar(diag_d[0:p, k, 0:p], id_sb[0:p, 0:p], one_plus_d[0:p, k:k + 1], None, ALU.mult)
            for half, p in ((0, 128), (1, D1)):
                dve.wait_ge(s_wd, half + 1)
                V.tensor_copy(w_delta[0:p, half, :], psum[0:p, half, 0:256]).then_inc(s_wds, 1)
            for part in range(4):
                states(0, 0, part)
                if part == 3:
                    for k in range(2):
                        tokens(1, 1, k)
            make_v(0, 0, 0)
            make_v(0, 0, 1)
            with dve.Fori(0, LOOPED // 2) as o2:
                for par in range(2):
                    octet(o2 * 2 + par, par, True, True)
            octet(OCTS - 2, 0, True, False)
            octet(OCTS - 1, 1, False, False)

            V.tensor_copy(id_r[:, :], id_sb[:, :])
            V.tensor_copy(pair_r[:, :], pair_sb[:, :])
            for par in range(2):
                V.tensor_copy(sh_rest[D1:D1 + 2, par, :], ones_sb[D1:D1 + 2, :])
            V.memset(comb[:, :, EXPERTS:NE], 1.0).then_inc(s_rest1, 1)
            dve.wait_ge(s_w2, 16 * N_W2)
            for k in range(2):
                V.tensor_copy(gate_r[:, 2 * k, :], gate_w_sb[:, k, :]).then_inc(s_gate, 1)
            dve.wait_ge(s_gate, 2)
            for k in range(2):
                V.tensor_tensor(gate_r[:, 2 * k + 1, :], gate_w_sb[:, k, :], gate_r[:, 2 * k, :].bitcast(F32),
                                ALU.subtract).then_inc(s_gate, 1)

            def statistics(j):
                for i in range(BT):
                    if i % 2 == 0:
                        dve.wait_ge(s_rtr, CREDIT + j * (BT // 2) + i // 2 + 1)
                    V.bn_stats(st6[:, i, :], psum[:, i // 2, i % 2 * D:(i % 2 + 1) * D]).then_inc(s_ln, 1)
                dve.wait_ge(s_idle, CREDIT + j)
                dve.wait_ge(s_ln, j * (2 * BT + 1) + BT)
                V.memset(idle[0:1, 0:1], 0.0).then_inc(s_idle, 1)
                for i in range(BT):
                    V.bn_aggr(mv[:, i, :], st6[:, i, :]).then_inc(s_ln, 1)
                dve.wait_ge(s_ln, j * (2 * BT + 1) + 2 * BT)
                V.tensor_scalar(mv_eps[:, :], mv[:, :, 1], 1e-5, None, ALU.add).then_inc(s_ln, 1)

            def normalise(j):
                dve.wait_ge(s_rstd, j + 1)
                for i in range(BT):
                    V.tensor_scalar(hn[:, i, 0:D], psum[:, i // 2, i % 2 * D:(i % 2 + 1) * D], mv[:, i, 0:1],
                                    rstd[:, i:i + 1], ALU.subtract, ALU.mult).then_inc(s_hn, 1)
                dve.wait_ge(s_hn, (j + 1) * BT)
                V.tensor_copy(hn[:, :, D:D + D1], hn[:, :, D0:D]).then_inc(s_dup, 1)

            def second_parts(j):
                cols = bass.ds(j * BW, BW) if not isinstance(j, int) else slice(j * BW, (j + 1) * BW)
                dve.wait_ge(s_hcopy, j * 2 + 1)
                V.tensor_tensor(h_lo[:, cols], flat[:, 3 * 512:3 * 512 + BW], h_hi[:, cols].bitcast(F32),
                                ALU.subtract).then_inc(s_hout, 1)
                dve.wait_ge(s_hcopy, j * 2 + 2)
                V.scalar_tensor_tensor(out=h_tail[:, cols], in0=tail_hi[:, :].bitcast(F32),
                                       scalar=vec[:, V_TAIL:V_TAIL + 1], in1=flat[:, 5 * 512:5 * 512 + BW],
                                       op0=ALU.mult, op1=ALU.add).then_inc(s_hout, 1)

            statistics(0)
            with dve.Fori(0, BATCHES - 1) as j:
                normalise(j)
                statistics(j + 1)
                second_parts(j)
            normalise(BATCHES - 1)
            second_parts(BATCHES - 1)

            steps = [0]

            def step(i):
                steps[0] += 1
                i.then_inc(s_gs, 1)
                dve.wait_ge(s_gs, steps[0])

            B3 = [128, TILES, EXPERTS]
            dve.wait_ge(s_gl, 1)
            turned = psum[:, 7, 0:TILES * EXPERTS].rearrange("p (t e) -> p t e", e=EXPERTS)
            step(V.tensor_reduce(row[:, :], turned, AX.X, ALU.max))
            step(V.tensor_tensor(score[:, :, :], turned, row[:, :].unsqueeze(2).to_broadcast(B3), ALU.subtract))
            dve.wait_ge(s_gx, 1)
            step(V.tensor_reduce(row[:, :], prob[:, :, :], AX.X, ALU.add))
            step(V.reciprocal(row[:, :], row[:, :]))
            step(V.tensor_tensor(prob[:, :, :], prob[:, :, :], row[:, :].unsqueeze(2).to_broadcast(B3), ALU.mult))
            step(V.tensor_tensor(score[:, :, :], prob[:, :, :],
                                 gate_b_sb[:, :].unsqueeze(1).to_broadcast(B3), ALU.add))
            step(V.tensor_tensor(g4[:, :, :], score[:, :, 0::2], score[:, :, 1::2], ALU.add))

            def rank(dst, s, n):
                mine = s.unsqueeze(3).to_broadcast([128, TILES, n, n])
                other = s.unsqueeze(2).to_broadcast([128, TILES, n, n])
                a, b = cmpa[:, :, 0:n, 0:n], cmpb[:, :, 0:n, 0:n]
                step(V.tensor_tensor(a, other, mine, ALU.is_equal))
                step(V.tensor_tensor(a, a, below_sb[:, 0:n, 0:n].unsqueeze(1).to_broadcast([128, TILES, n, n]),
                                     ALU.mult))
                step(V.tensor_tensor(b, other, mine, ALU.is_gt))
                step(V.tensor_tensor(a, a, b, ALU.add))
                step(V.tensor_reduce(dst, a, AX.X, ALU.add))

            rank(r4[:, :, :], g4[:, :, :], 4)
            step(V.tensor_scalar(k4[:, :, :], r4[:, :, :], 2.0, -BIG, ALU.is_ge, ALU.mult))
            grouped = score.rearrange("p t (g k) -> p t g k", k=2)
            step(V.tensor_tensor(grouped, grouped, k4[:, :, :].unsqueeze(3).to_broadcast([128, TILES, 4, 2]), ALU.add))
            for k in range(2):
                mine = mark if k else keep8
                step(V.tensor_reduce(row[:, :], score[:, :, :], AX.X, ALU.max))
                step(V.tensor_tensor(mine[:, :, :], score[:, :, :], row[:, :].unsqueeze(2).to_broadcast(B3),
                                     ALU.is_equal))
                step(V.tensor_tensor(mine[:, :, :], mine[:, :, :],
                                     below_sb[:, EXPERTS:, :].to_broadcast(B3), ALU.mult))
                step(V.tensor_reduce(last[:, :], mine[:, :, :], AX.X, ALU.max))
                step(V.tensor_tensor(mine[:, :, :], mine[:, :, :], last[:, :].unsqueeze(2).to_broadcast(B3),
                                     ALU.is_equal))
                if k == 0:
                    step(V.scalar_tensor_tensor(out=score[:, :, :], in0=keep8[:, :, :], scalar=-4.0 * BIG,
                                                in1=score[:, :, :], op0=ALU.mult, op1=ALU.add))
            step(V.tensor_tensor(keep8[:, :, :], keep8[:, :, :], mark[:, :, :], ALU.add))
            step(V.tensor_tensor(comb[:, :, 0:EXPERTS], keep8[:, :, :], prob[:, :, :], ALU.mult))

            def group(t, par, q):
                n = (par + q) % 2
                b0 = n * GRP
                k = t * GRPS + q
                dve.wait_ge(s_h3, k + 1)
                V.tensor_tensor(prod[:, n].rearrange("p w (e i) -> p e w i", e=GRP),
                                psum[:, b0:b0 + GRP, 0:2 * HID].rearrange("p e (w i) -> p e w i", w=2),
                                h3[:, n].rearrange("p e (w i) -> p e w i", w=2), ALU.mult).then_inc(s_prod, 1)
                dve.wait_ge(s_prod, k + 1)
                V.tensor_scalar(xg[:, n, :], prod[:, n, 0, :], 7.0, None, ALU.min).then_inc(s_clip, 1)
                V.tensor_scalar(xl[:, n, :], prod[:, n, 1, :], -7.0, 7.0, ALU.max, ALU.min).then_inc(s_clip, 1)
                dve.wait_ge(s_clip, k * 2 + 2)
                V.scalar_tensor_tensor(out=xa[:, n, :], in0=xl[:, n, :], scalar=1.0, in1=xg[:, n, :],
                                       op0=ALU.add, op1=ALU.mult).then_inc(s_xa, 1)
                dve.wait_ge(s_xa, k + 1)
                dve.wait_ge(s_sig, k + 1)
                for e in range(GRP):
                    x = q * GRP + e
                    own = slice(e * HID, (e + 1) * HID)
                    i = V.scalar_tensor_tensor(out=g[:, par, x * HID:(x + 1) * HID], in0=xa[:, n, own],
                                               scalar=wt[:, par, x:x + 1], in1=sg[:, n, own],
                                               op0=ALU.mult, op1=ALU.mult)
                i.then_inc(s_g, 1)

            def norm_out(t, par):
                dve.wait_ge(s_op, CREDIT + t + 1)
                V.bn_stats(o6[:, :], psum[:, 7, 0:D]).then_inc(s_ostat, 1)
                dve.wait_ge(s_ostat, t * 3 + 1)
                dve.wait_ge(s_idle, CREDIT + t + BATCHES)
                V.memset(idle[0:1, 0:1], 0.0).then_inc(s_idle, 1)
                V.bn_aggr(omv[:, par, :], o6[:, :]).then_inc(s_ostat, 1)
                dve.wait_ge(s_ostat, t * 3 + 2)
                V.tensor_scalar(oeps[:, par:par + 1], omv[:, par, 1:2], 1e-5, None, ALU.add).then_inc(s_ostat, 1)
                dve.wait_ge(s_orstd, t + 1)
                dve.wait_ge(s_out, CREDIT_DMA + t * 16)
                V.tensor_scalar(ot[:, par, :], psum[:, 7, 0:D], omv[:, par, 0:1], orstd[:, par:par + 1],
                                ALU.subtract, ALU.mult).then_inc(s_ot, 1)

            def tile(t, par, before):
                cols = bass.ds(t, 1) if not isinstance(t, int) else slice(t, t + 1)
                V.tensor_copy(wt[:, par, :], comb[:, cols, :].rearrange("p o e -> p (o e)")).then_inc(s_wt, 1)
                dve.wait_ge(s_wt, t + 1)
                if before:
                    dve.wait_ge(s_gtr, CREDIT + t * 2 - 2)
                V.tensor_copy(g[:, par, NE * HID:GK], wt[:, par, :])
                for q in range(GRPS):
                    group(t, par, q)
                if before:
                    norm_out(t - 1, 1 - par)

            tile(0, 0, False)
            with dve.Fori(0, TILES // 2 - 1) as t2:
                for j in range(2):
                    tile(t2 * 2 + 1 + j, 1 - j, True)
            tile(TILES - 1, 1, True)
            norm_out(TILES - 1, 1)


def kernel(**inputs):
    import numpy as _np
    import concourse.bacc as _bacc
    from concourse import mybir as _mybir
    from concourse.bass_utils import run_bass_kernel_spmd as _run

    x = {k: _np.asarray(a) for k, a in inputs.items()}

    def padded(a, shape):
        z = _np.zeros(shape, a.dtype)
        z[tuple(slice(0, n) for n in a.shape)] = a
        return z

    def low_high(a, twice=False):
        z = _np.zeros((128, 2, a.shape[1]), a.dtype)
        z[:, 0], z[:D1, 1] = a[:D0], a[D0:]
        if twice:
            z[D1:, 1] = a[D0:]
        return z

    im = x["x"].reshape(OCTS, OCT, 6, 16, 6, 48).transpose(0, 3, 5, 1, 2, 4).reshape(OCTS, KC, 128, OCT, PATCHES)
    patches = _np.zeros((OCTS, 128, KC, OCT, SLOT), im.dtype)
    patches[..., 1:] = im.transpose(0, 2, 1, 3, 4)
    patches = patches.reshape(OCTS, 128, KC, W)
    wt = x["L0_tok_W"].reshape(KC, 128, D).transpose(1, 0, 2)
    w_tok = _np.concatenate([wt, wt[:, :, D0:]], axis=2)
    col = lambda n: low_high(x[n][:, None], True)[:, :, 0]
    a_log = low_high(x["L0_attn_A_log"], True)
    a_high = _np.concatenate([a_log[:D1, 1, 0::2], a_log[:D1, 1, 1::2]], axis=0)
    marks = _np.zeros((128, 2), _np.float32)
    marks[:D1, 0] = marks[D1 + 1, 0] = 1.0
    marks[D1:, 1] = -1.0
    vecs = _np.concatenate([a_log[:, 0], a_high, col("L0_attn_b_dt"), col("L0_attn_rms_scale"),
                            col("L0_attn_D_param"), col("L0_tok_b"), marks], axis=1)
    pos = _np.zeros((128, 2, SLOT), _np.float32)
    pos[:, :, 1:] = low_high(_np.ascontiguousarray(x["L0_tok_pos_emb"].T), True)
    w_bc = low_high(_np.concatenate([x["L0_attn_W_bc"]] * 2, axis=1))
    w_dt = _np.concatenate([x["L0_attn_W_dt"].T, x["L0_attn_W_dt"].T[:, D0:]], axis=1)
    w_dtp = _np.concatenate([x["L0_attn_W_dtp"], x["L0_attn_W_dtp"][:, D0:]], axis=1)
    ident = _np.eye(128, dtype=_np.float32)
    pair_ident = _np.concatenate([ident[:D1, :D1]] * 2, axis=0)
    pick = _np.concatenate([ident[:32, :32]] * 2, axis=0)
    pick[:, :16] *= _np.float32(0.25)
    gate_w = low_high(_np.ascontiguousarray(x["L0_ffn_gate_w"].T), True)
    gate_b = _np.ascontiguousarray(_np.broadcast_to(x["L0_ffn_gate_b"], (128, EXPERTS)))
    below = _np.concatenate([_np.tri(EXPERTS, EXPERTS, -1, dtype=_np.float32),
                             _np.arange(EXPERTS, 0, -1, dtype=_np.float32)[None]], axis=0)
    below = _np.ascontiguousarray(_np.broadcast_to(below, (128,) + below.shape))

    def halves(w, ws):
        w = _np.concatenate([w, ws[None]], axis=0)
        return _np.concatenate([w[..., 0::2], w[..., 1::2]], axis=-1)

    w13 = _np.concatenate([halves(x["L0_ffn_W1"], x["L0_ffn_Ws1"]), halves(x["L0_ffn_W3"], x["L0_ffn_Ws3"])], axis=-1)
    b13 = _np.concatenate([halves(x["L0_ffn_B1"], x["L0_ffn_Bs1"]), halves(x["L0_ffn_B3"], x["L0_ffn_Bs3"])], axis=-1)
    groups = lambda a: a.reshape(GRPS, GRP, -1, 4 * HID).transpose(0, 2, 1, 3)
    w13_tail = _np.concatenate([w13[:, D0:]] * 2, axis=1)
    w13_rest = _np.concatenate([w13[:, D0:], b13[:, None], b13[:, None]], axis=1)
    w2 = _np.concatenate([x["L0_ffn_W2"].reshape(-1, D), x["L0_ffn_Ws2"], x["L0_ffn_B2"], x["L0_ffn_Bs2"][None]], axis=0)
    w2 = padded(w2, (GC * 128, D)).reshape(GC, 128, D).transpose(1, 0, 2)
    laid = {"patches": patches, "w_tok": w_tok, "vecs": vecs, "pos": pos, "w_bc": w_bc, "w_dt": w_dt, "w_dtp": w_dtp,
            "ident": ident, "pair_ident": pair_ident, "bc_pick": pick,
            "gate_w": gate_w, "gate_b": gate_b,
            "below": below, "w13_low": groups(w13[:, :D0]), "w13_tail": groups(w13_tail),
            "w13_rest": groups(w13_rest), "w2": w2}

    nc = _bacc.Bacc("TRN2", target_bir_lowering=False, num_devices=1)
    arrays, args = {}, []
    for name, a in laid.items():
        a = _np.ascontiguousarray(a)
        arrays[f"in_{name}_dram"] = a
        args.append(nc.dram_tensor(f"in_{name}_dram", a.shape, _mybir.dt.from_np(a.dtype), kind="ExternalInput").ap())
    out = nc.dram_tensor("out_0_dram", (IMAGES, PATCHES, D), _mybir.dt.float32, kind="ExternalOutput").ap()
    vit_tower(nc, *args, out)
    r = _run(nc, [arrays], core_ids=[0])
    return r.results[0]["out_0_dram"]
```
